# Optimizing a Trainium2 kernel written in Bass

```python
import numpy as np
import jax
import jax.numpy as jnp

def _softmax(x, axis=-1):
    return jax.nn.softmax(x, axis=axis)

def _gelu(x):
    return jax.nn.gelu(x, approximate=True)

def _silu(x):
    return jax.nn.silu(x)

def _sigmoid(x):
    return jax.nn.sigmoid(x)

def _layernorm(x, axis=-1, eps=1e-05):
    m = jnp.mean(x, axis=axis, keepdims=True)
    v = jnp.var(x, axis=axis, keepdims=True)
    return (x - m) / jnp.sqrt(v + eps)

def _scatter_add(tgt, idx, src, axis=0):
    return tgt.at[idx].add(src)

def _segment_sum(src, seg, n):
    return jax.ops.segment_sum(src, seg, n)
kernel_name = 'mk_adj_preln_d2_adj_r2_e7601d'

def setup_inputs(seed: int=0):
    np.random.seed(seed)
    _w = jnp.asarray

    def _rec_inputs():
        import jax
        import jax.numpy as jnp
        _gk = jax.random.key(seed)
        x = 7.22e-05 + 1 * jax.random.normal(jax.random.fold_in(_gk, 1), (16, 512, 256), jnp.float32)
        _a = jax.random.bernoulli(jax.random.fold_in(_gk, 2), 0.0078125, (512, 512))
        _a = jnp.logical_or(_a, jnp.swapaxes(_a, -1, -2))
        _a = jnp.logical_or(_a, jnp.eye(512, dtype=bool))
        adj = _a.astype(jnp.int32)
        return (x, adj)
    x, adj = _rec_inputs()

    def _L0_gnn_setup():
        import jax, jax.numpy as jnp
        import numpy as np
        LEAKY_ALPHA = 0.01
        NEG_INF = -1000000000.0
        LN_EPS = 1e-05

        def _gat_heads(x, adj, W, a):
            O = W.shape[-1]
            Wh = jnp.einsum('bnf,hfo->bhno', x, W)
            f1 = jnp.einsum('bhno,ho->bhn', Wh, a[:, :O])
            f2 = jnp.einsum('bhno,ho->bhn', Wh, a[:, O:])
            e = f1[:, :, :, None] + f2[:, :, None, :]
            e = jnp.where(e > 0, e, LEAKY_ALPHA * e)
            e = jnp.where(adj[None, None] > 0, e, NEG_INF)
            attn = jax.nn.softmax(e, axis=-1)
            return jnp.einsum('bhnm,bhmo->bhno', attn, Wh)
        key = jax.random.key(seed)
        ks = jax.random.split(key, 10)
        B, N, F_in, F_hid, H, F_out, D_ff = (8, 1024, 256, 256, 4, 256, 256)
        s = 0.05
        return {'enc_inputs': jax.random.normal(ks[0], (B, N, F_in), jnp.float32), 'adj': jax.random.randint(ks[1], (N, N), 0, 2, jnp.int32), 'W_heads': jax.random.normal(ks[2], (H, F_in, F_hid), jnp.float32) * s, 'a_heads': jax.random.normal(ks[3], (H, 2 * F_hid), jnp.float32) * s, 'W_out': jax.random.normal(ks[4], (H * F_hid, F_out), jnp.float32) * s, 'a_out': jax.random.normal(ks[5], (2 * F_out,), jnp.float32) * s, 'w1': jax.random.normal(ks[6], (F_out, D_ff), jnp.float32) * s, 'b1': jnp.zeros((D_ff,), jnp.float32), 'w2': jax.random.normal(ks[7], (D_ff, F_out), jnp.float32) * s, 'b2': jnp.zeros((F_out,), jnp.float32), 'ln_gamma': jnp.ones((F_out,), jnp.float32), 'ln_beta': jnp.zeros((F_out,), jnp.float32)}
    _L0_gnn_all = _L0_gnn_setup()
    _L0_gnn_in = {k: v for k, v in _L0_gnn_all.items() if k in ('W_heads', 'a_heads', 'W_out', 'a_out', 'w1', 'b1', 'w2', 'b2', 'ln_gamma', 'ln_beta')}
    del _L0_gnn_all

    def _L1_gnn_setup():
        import jax, jax.numpy as jnp
        import numpy as np
        B, K, DIN, DOUT = (32, 64, 256, 256)
        key = jax.random.key(seed)
        k1, k2, k3, k4 = jax.random.split(key, 4)
        x = jax.random.normal(k1, (B, K, DIN), dtype=jnp.float32)
        adj = jax.random.randint(k2, (K, K), 0, 2, dtype=jnp.int32)
        W = jax.random.normal(k3, (DOUT, 2 * DIN), dtype=jnp.float32) * 0.02
        b = jax.random.normal(k4, (DOUT,), dtype=jnp.float32) * 0.02
        return {'x': x, 'adj': adj, 'W': W, 'b': b}
    _L1_gnn_all = _L1_gnn_setup()
    _L1_gnn_in = {k: v for k, v in _L1_gnn_all.items() if k in ('W', 'b')}
    del _L1_gnn_all
    return {'x': x, 'adj': adj, 'L0_gnn_W_heads': _L0_gnn_in['W_heads'], 'L0_gnn_a_heads': _L0_gnn_in['a_heads'], 'L0_gnn_W_out': _L0_gnn_in['W_out'], 'L0_gnn_a_out': _L0_gnn_in['a_out'], 'L0_gnn_w1': _L0_gnn_in['w1'], 'L0_gnn_b1': _L0_gnn_in['b1'], 'L0_gnn_w2': _L0_gnn_in['w2'], 'L0_gnn_b2': _L0_gnn_in['b2'], 'L0_gnn_ln_gamma': _L0_gnn_in['ln_gamma'], 'L0_gnn_ln_beta': _L0_gnn_in['ln_beta'], 'L1_gnn_W': _L1_gnn_in['W'], 'L1_gnn_b': _L1_gnn_in['b']}

def reference(x, adj, L0_gnn_W_heads, L0_gnn_a_heads, L0_gnn_W_out, L0_gnn_a_out, L0_gnn_w1, L0_gnn_b1, L0_gnn_w2, L0_gnn_b2, L0_gnn_ln_gamma, L0_gnn_ln_beta, L1_gnn_W, L1_gnn_b):
    import jax
    import jax.numpy as jnp

    def _L0_gnn_ref(enc_inputs, adj, W_heads, a_heads, W_out, a_out, w1, b1, w2, b2, ln_gamma, ln_beta):
        import jax, jax.numpy as jnp
        import numpy as np
        LEAKY_ALPHA = 0.01
        NEG_INF = -1000000000.0
        LN_EPS = 1e-05

        def _gat_heads(x, adj, W, a):
            O = W.shape[-1]
            Wh = jnp.einsum('bnf,hfo->bhno', x, W)
            f1 = jnp.einsum('bhno,ho->bhn', Wh, a[:, :O])
            f2 = jnp.einsum('bhno,ho->bhn', Wh, a[:, O:])
            e = f1[:, :, :, None] + f2[:, :, None, :]
            e = jnp.where(e > 0, e, LEAKY_ALPHA * e)
            e = jnp.where(adj[None, None] > 0, e, NEG_INF)
            attn = jax.nn.softmax(e, axis=-1)
            return jnp.einsum('bhnm,bhmo->bhno', attn, Wh)
        B, N, _ = enc_inputs.shape
        h = jax.nn.elu(_gat_heads(enc_inputs, adj, W_heads, a_heads))
        h = jnp.transpose(h, (0, 2, 1, 3)).reshape(B, N, -1)
        out = _gat_heads(h, adj, W_out[None], a_out[None])[:, 0]
        out = jax.nn.elu(out)
        ffn = jnp.maximum(out @ w1 + b1, 0.0) @ w2 + b2
        y = ffn + out
        mu = jnp.mean(y, axis=-1, keepdims=True)
        var = jnp.var(y, axis=-1, keepdims=True)
        return (y - mu) / jnp.sqrt(var + LN_EPS) * ln_gamma + ln_beta

    def _L1_gnn_ref(x, adj, W, b):
        import jax, jax.numpy as jnp
        import numpy as np
        B, K, DIN, DOUT = (32, 64, 256, 256)
        Din = x.shape[-1]
        Wi, Wj = (W[:, :Din], W[:, Din:])
        mi = jnp.einsum('bkd,od->bko', x, Wi)
        mj = jnp.einsum('bkd,od->bko', x, Wj)
        a = adj.astype(x.dtype)
        deg = a.sum(axis=1)
        out = deg[None, :, None] * (mi + b) + jnp.einsum('ij,bjo->bio', a, mj)
        return out
    h = jnp.maximum(_layernorm(x, axis=-1), 0.0)
    x = x + _L0_gnn_ref(h, adj, L0_gnn_W_heads, L0_gnn_a_heads, L0_gnn_W_out, L0_gnn_a_out, L0_gnn_w1, L0_gnn_b1, L0_gnn_w2, L0_gnn_b2, L0_gnn_ln_gamma, L0_gnn_ln_beta)
    h = jnp.maximum(_layernorm(x, axis=-1), 0.0)
    x = x + _L1_gnn_ref(h, adj, L1_gnn_W, L1_gnn_b)
    return x

_drawn_inputs = setup_inputs


def setup_inputs(seed=0):
    import zlib

    import numpy as np

    out = dict(_drawn_inputs(seed))
    spreads = {'L0_gnn_b1': (0.0, 0.1),
     'L0_gnn_b2': (0.0, 0.1),
     'L0_gnn_ln_gamma': (1.0, 0.2),
     'L0_gnn_ln_beta': (0.0, 0.1)}
    factors = {'L0_gnn_a_out': 3.737}
    for name, (base, spread) in spreads.items():
        noise = np.random.default_rng([zlib.crc32(name.encode()), seed]).standard_normal(out[name].shape)
        drawn = base * np.exp(spread * noise) if base else spread * noise
        out[name] = jnp.asarray(drawn.astype(out[name].dtype))
    for name, factor in factors.items():
        out[name] = (out[name] * factor).astype(out[name].dtype)
    return out
```

```python
from contextlib import ExitStack

import concourse.bass as bass
from concourse import mybir

F32 = mybir.dt.float32
F32R = mybir.dt.float32r
BF16 = mybir.dt.bfloat16
I32 = mybir.dt.int32
ALU = mybir.AluOpType
ACT = mybir.ActivationFunctionType
AX_X = mybir.AxisListType.X

P = 128
EPS = 1e-5
SLOPE = 0.01
MASKED = -1e30
LOWEST = -3e38
SLOTS = 5
SCORE_BUFFER = (0, 1, 0, 1, 2)

GEN_USES = {
    "value2": (0, True), "ffn2": (-2, False), "bcast_out": (-1, False),
    "value3": (0, True), "h0T": (1, True), "bcast3": (0, False),
    "frows": (1, True), "AH": (-2, True), "bcast0": (1, False),
    "value0": (1, True), "DH": (-2, True), "L1": (-2, False), "bcast1": (1, False),
    "value1": (1, True), "ffn1": (-1, True), "bcast2": (1, False),
}
BROADCAST_FOR = {"bcast_out": 2, "bcast3": 3, "bcast0": 4, "bcast1": 5, "bcast2": 6}
UNIT_BATCH = (0, 0, -1, 0, 1)
HEAD_OF = (1, 2, None, 3, 0)
FIRST_STEP, LOOP_FROM = -1, 2


class Tally:

    def __init__(self, offsets, batches):
        self.offsets, self.batches = dict(offsets), batches

    def _has(self, t, name):
        return 0 <= t + self.offsets[name] < self.batches

    def after(self, t, name):
        names = list(self.offsets)
        at = names.index(name) + 1
        if isinstance(t, int):
            before = sum(self._has(s, n) for s in range(FIRST_STEP, t) for n in names)
            return before + sum(self._has(t, n) for n in names[:at])
        before = sum(self._has(s, n) for s in range(FIRST_STEP, LOOP_FROM) for n in names)
        return (t - LOOP_FROM) * len(names) + (before + at)


def build(nc, x, adj, W_heads, a_heads, W_out, a_out, w1, b1, w2, b2, gamma, beta, L1_W, L1_b, out):
    B, N, F = x.shape
    H, _, O = W_heads.shape
    assert F == O == 256 and N == 512 and H == 4
    NT, FT = N // P, F // P
    GEN = Tally({n: o for n, (o, _) in GEN_USES.items()}, B)
    GEN_EVAC = Tally({n: o for n, (o, _) in GEN_USES.items() if not n.startswith("bcast") and n != "L1"}, B)
    GEN_HI = Tally({n: o for n, (o, pair) in GEN_USES.items() if pair}, B)
    UNIT = Tally(enumerate(UNIT_BATCH), B)

    def unit_no(t, slot):
        while slot >= SLOTS:
            t, slot = t + 1, slot - SLOTS
        while slot < 0:
            t, slot = t - 1, slot + SLOTS
        return UNIT.after(t, slot)

    def exists(t, offset):
        return not isinstance(t, int) or 0 <= t + offset < B

    def has_unit(t, slot):
        while slot >= SLOTS:
            t, slot = t + 1, slot - SLOTS
        while slot < 0:
            t, slot = t - 1, slot + SLOTS
        return exists(t, UNIT_BATCH[slot])

    def wait(eng, sem, value):
        if not isinstance(value, int) or value > 0:
            eng.wait_ge(sem, value)

    def wait_apart(eng, sem, value, reached):
        if not isinstance(value, int):
            eng.compute_val(value)
        eng.wait_ge(reached, 1)
        wait(eng, sem, value)

    def steps(eng, step):
        for t in range(FIRST_STEP, LOOP_FROM):
            step(t)
        with eng.Fori(LOOP_FROM, B - 2) as t:
            step(t)
        for t in range(B - 2, B + 2):
            step(t)

    with ExitStack() as ctx:
        def sb(name, shape, dt=F32):
            return ctx.enter_context(nc.sbuf_tensor(name, shape, dt))

        def sem(name):
            return ctx.enter_context(nc.semaphore(name))

        ps_turn = ctx.enter_context(nc.psum_tensor("ps_turn", [P, 2, 512], F32))
        ps_z = ctx.enter_context(nc.psum_tensor("ps_z", [P, FT, 512], F32))
        ps_acc = ctx.enter_context(nc.psum_tensor("ps_acc", [P, NT, O], F32))
        ps_gen = ctx.enter_context(nc.psum_tensor("ps_gen", [P, 2, 512], F32))
        gen_flat = ps_gen[:, :, :].rearrange("p a b -> p (a b)")
        gen_rows = gen_flat.rearrange("p (n o) -> p n o", o=O)
        bcast = ps_gen[:, 1, :]

        W_hl = sb("W_hl", [P, 2, FT, H * O], F32R)
        Wout_hl = sb("Wout_hl", [P, 2, H * FT, O], F32R)
        w1_hl = sb("w1_hl", [P, 2, FT, O], F32R)
        w2_hl = sb("w2_hl", [P, 2, FT, O], F32R)
        wij_hl = sb("wij_hl", [P, 2, 2, FT, O], F32R)
        wa_hl = sb("wa_hl", [P, 2, FT, 2 * H], F32R)
        wa = sb("wa", [P, FT, 2 * H])
        adjT = sb("adjT", [P, NT, N], F32R)
        mask = sb("mask", [P, NT, N], BF16)
        deg = sb("deg", [P, NT])
        deg_diag = sb("deg_diag", [P, NT, P], F32R)
        select = sb("select", [40, H, P], F32R)
        ident = sb("ident", [P, P])
        ident_r = sb("ident_r", [P, P], F32R)
        ones = sb("ones", [P, P])
        b1_col = sb("b1_col", [P, FT])
        b2_row = sb("b2_row", [P, O])
        gamma_row = sb("gamma_row", [P, O])
        beta_row = sb("beta_row", [P, O])
        bL_row = sb("bL_row", [P, O])
        aout_row = sb("aout_row", [P, 2, O])
        minus_half = sb("minus_half", [P, NT])

        xin = sb("xin", [P, NT, F])
        h0T = sb("h0T", [P, 2, FT, N], F32R)
        frow = sb("frow", [2 * H, N])
        frow_hl = sb("frow_hl", [40, N], F32R)
        f1 = sb("f1", [P, NT, 2 * H])
        value = sb("value", [P, 2, 2, NT, O], F32R)
        value_out = sb("value_out", [P, 2, NT, O], F32R)
        f_out = sb("f_out", [P, 2, NT])
        f2_diag = sb("f2_diag", [P, NT, P])
        selectf = f2_diag[0:40, :, :]
        scratch = sb("scratch", [P, 2, O])

        score = [sb(f"score{i}", [P, NT, N]) for i in range(3)]
        rowmax = sb("rowmax", [P, SLOTS, NT])
        negmax = sb("negmax", [P, SLOTS, NT])
        rowsum = sb("rowsum", [P, SLOTS, NT])
        rinv = sb("rinv", [P, SLOTS, NT])
        probT = sb("probT", [P, 2, 2, N], F32R)
        elu = sb("elu", [P, FT * N])
        zT = sb("zT", [P, 2, 2, FT * N], F32R)
        oT = sb("oT", [P, 2, FT * N], F32R)

        rT = sb("rT", [P, 2, FT * N], F32R)
        dhT = value_out[:, :, :, :].rearrange("p s n o -> p s (n o)")
        y = sb("y", [P, NT, O])
        xres = sb("xres", [P, NT, F])
        rF = xres[:, :, :].rearrange("p n f -> p (n f)")
        h1f = sb("h1f", [P, NT, O])
        h1 = sb("h1", [P, 2, NT, O], F32R)
        bn = sb("bn", [P, 3, NT, 6])
        mv = sb("mv", [P, 3, NT, 2])
        veps = sb("veps", [P, 3, NT])
        rstd = sb("rstd", [P, 3, NT])
        nmr = sb("nmr", [P, 3, NT])

        ld_x, ld_xres, st_out = sem("ld_x"), sem("ld_xres"), sem("st_out")
        ld_W, ld_a, ld_adj, ld_Wout, ld_L1, ld_small = (
            sem("ld_W"), sem("ld_a"), sem("ld_adj"), sem("ld_Wout"), sem("ld_L1"), sem("ld_small"))
        SMALL_LOADS, CONSTS = 8, 5
        zeroed, ident_ready, const_ready = sem("zeroed"), sem("ident_ready"), sem("const_ready")
        adj_float, mask_ready, deg_ready, adj_turned, L1_turned = (
            sem("adj_float"), sem("mask_ready"), sem("deg_ready"), sem("adj_turned"), sem("L1_turned"))
        wa_ready, halves_hi, halves_lo, exact_ready = (
            sem("wa_ready"), sem("halves_hi"), sem("halves_lo"), sem("exact_ready"))
        gen_ready, gen_hi, gen_evacuated = sem("gen_ready"), sem("gen_hi"), sem("gen_evacuated")
        logits_ready, leaky_ready, masked_ready = sem("logits_ready"), sem("leaky_ready"), sem("masked_ready")
        negmax_ready, exp_done, rinv_ready, probs_ready = (
            sem("negmax_ready"), sem("exp_done"), sem("rinv_ready"), sem("probs_ready"))
        turned, turned_hi, turned_lo, chunk_used = sem("turned"), sem("turned_hi"), sem("turned_lo"), sem("chunk_used")
        z_ready, z_relu, z_exp, elu_ready, z_hi, z_lo = (
            sem("z_ready"), sem("z_relu"), sem("z_exp"), sem("elu_ready"), sem("z_hi"), sem("z_lo"))
        acc_used, acc_hi, acc_lo, fout_ready, fdiag_ready = (
            sem("acc_used"), sem("acc_hi"), sem("acc_lo"), sem("fout_ready"), sem("fdiag_ready"))
        frow_ready, f1_ready = sem("frow_ready"), sem("f1_ready")
        stats, veps_ready, rstd_ready, nmr_ready = (
            [sem(f"{n}{i}") for i in range(3)] for n in ("stats", "veps_ready", "rstd_ready", "nmr_ready"))
        h0_ready, relu_ready, y_ready, ynorm_ready, ygamma, x1_ready, xb_ready = (
            sem("h0_ready"), sem("relu_ready"), sem("y_ready"), sem("ynorm_ready"), sem("ygamma"),
            sem("x1_ready"), sem("xb_ready"))
        h1_ready, h1_hi, h1_lo, x1b_ready, out_ready = (
            sem("h1_ready"), sem("h1_hi"), sem("h1_lo"), sem("x1b_ready"), sem("out_ready"))

        x_tiles = x.rearrange("b (n p) f -> b p n f", p=P)
        out_tiles = out.rearrange("b (n p) f -> b p n f", p=P)

        def row(v):
            return v.rearrange("(a n) -> a n", a=1).broadcast_to((P, v.shape[0]))

        def flat(ap):
            return ap.rearrange("p a b -> p (a b)")

        def hl(t, *at):
            return [flat(t[(slice(None), i, *at)]) if not at else flat(t[:, i, at[0], :, :]) for i in range(2)]

        SPLITS = [
            (hl(W_hl), flat(score[0][:, :, :]), ld_W, 16 * FT),
            (hl(Wout_hl), flat(score[1][:, :, :]), ld_Wout, 16),
            (hl(w1_hl), flat(y[:, 0:2, :]), ld_small, 16 * SMALL_LOADS),
            (hl(w2_hl), flat(y[:, 2:4, :]), ld_small, 16 * SMALL_LOADS),
            (hl(wij_hl, 0), ps_gen[:, 0, :], L1_turned, 1),
            (hl(wij_hl, 1), ps_gen[:, 1, :], L1_turned, 1),
            (hl(wa_hl), flat(wa[:, :, :]), wa_ready, 2 * FT * H),
        ]
        HALVES = len(SPLITS)

        block = ctx.enter_context(nc.Block())

        @block.sync
        def _(sp):
            sp.dma_start(xin[:, :, :], x_tiles[0]).then_inc(ld_x, 16)
            for k in range(FT):
                sp.dma_start(flat(score[0][:, :, :])[:, k * H * O:(k + 1) * H * O].rearrange("p (h o) -> p h o", o=O),
                             W_heads[:, k * P:(k + 1) * P, :].rearrange("h p o -> p h o")).then_inc(ld_W, 16)
            sp.dma_start(elu[:, :], row(a_heads[0:2, :].rearrange("h o -> (h o)"))).then_inc(ld_a, 16)
            sp.dma_start(h1f[:, :, :].rearrange("p n o -> p (n o)"),
                         row(a_heads[2:4, :].rearrange("h o -> (h o)"))).then_inc(ld_a, 16)
            sp.dma_start(score[2][:, :, :].bitcast(I32), adj.rearrange("(n p) j -> p n j", p=P)).then_inc(ld_adj, 16)
            sp.dma_start(score[1][:, :, :].rearrange("p a (b o) -> p (a b) o", o=O),
                         W_out.rearrange("(k p) o -> p k o", p=P)).then_inc(ld_Wout, 16)
            sp.dma_start(xres[:, :, :].rearrange("p (c a) o -> p c (a o)", c=FT),
                         L1_W.rearrange("(c p) d -> p c d", p=P)).then_inc(ld_L1, 16)
            sp.dma_start(y[:, 0:2, :], w1.rearrange("(k p) o -> p k o", p=P)).then_inc(ld_small, 16)
            sp.dma_start(y[:, 2:4, :], w2.rearrange("(k p) o -> p k o", p=P)).then_inc(ld_small, 16)
            with nc.allow_non_contiguous_dma(reason="one bias, once"):
                sp.dma_start(b1_col[:, :], b1.rearrange("(k p) -> p k", p=P)).then_inc(ld_small, 16)
            for dst, src in ((b2_row, b2), (gamma_row, gamma), (beta_row, beta), (bL_row, L1_b)):
                sp.dma_start(dst[:, :], row(src)).then_inc(ld_small, 16)
            sp.dma_start(aout_row[:, :, :].rearrange("p a o -> p (a o)"), row(a_out)).then_inc(ld_small, 16)

            def step(t):
                if exists(t, -2):
                    wait(sp, x1_ready, t - 2)
                    sp.wait_ge(gen_evacuated, GEN_EVAC.after(t - 1, "ffn1"))
                    sp.wait_ge(L1_turned, 1)
                    sp.dma_start(xres[:, :, :], x_tiles[t - 2]).then_inc(ld_xres, 16)
                if exists(t, 2):
                    sp.wait_ge(gen_ready, GEN.after(t, "h0T"))
                    sp.dma_start(xin[:, :, :], x_tiles[t + 2]).then_inc(ld_x, 16)
                if exists(t, -2):
                    sp.wait_ge(out_ready, t - 1)
                    sp.dma_start(out_tiles[t - 2], h1f[:, :, :]).then_inc(st_out, 16)

            steps(sp, step)
            sp.wait_ge(st_out, 16 * B)

        @block.tensor
        def _(pe):
            mm = nc.tensor.matmul

            def split3(dst, stat, mov, first, last, **kw):
                mm(dst, stat[1], mov[0], start=first, stop=False, **kw)
                mm(dst, stat[0], mov[1], start=False, stop=False, **kw)
                return mm(dst, stat[0], mov[0], start=False, stop=last, **kw)

            def halves(ap_of):
                return ap_of(0), ap_of(1)

            def gen_claim(t, use):
                names = list(GEN_USES)
                s, at = t, names.index(use)
                while True:
                    at -= 1
                    if at < 0:
                        s, at = s - 1, len(names) - 1
                    if isinstance(s, int) and s < FIRST_STEP:
                        return
                    if exists(s, GEN_USES[names[at]][0]):
                        break
                before = names[at]
                if before in BROADCAST_FOR:
                    pe.wait_ge(logits_ready, 4 * unit_no(s, BROADCAST_FOR[before]))
                elif before == "L1":
                    pe.wait_ge(out_ready, s - 1)
                else:
                    pe.wait_ge(gen_evacuated, GEN_EVAC.after(s, before))

            pe.wait_ge(ident_ready, 1)
            pe.wait_ge(adj_float, 1)
            for j in range(NT):
                bank = (ps_turn, ps_z)[j // 2][:, j % 2, :]
                for i in range(NT):
                    last = nc.tensor.transpose(bank[:, i * P:(i + 1) * P], score[2][:, i, j * P:(j + 1) * P], ident[:, :])
                last.then_inc(adj_turned, 1)
            pe.wait_ge(ld_L1, 16)
            lw = xres[:, :, :].rearrange("p (c a) o -> p c (a o)", c=FT)
            for m in range(2):
                for d in range(FT):
                    for c in range(FT):
                        last = nc.tensor.transpose(ps_gen[:, m, d * O + c * P:d * O + (c + 1) * P],
                                                   lw[:, c, m * F + d * P:m * F + (d + 1) * P], ident[:, :])
            last.then_inc(L1_turned, 1)

            def turn(t, slot, c):
                n = unit_no(t, slot)
                if c == 0:
                    pe.wait_ge(probs_ready, 4 * n)
                wait(pe, turned_lo, 4 * (n - 1) + c - 1)
                p = score[SCORE_BUFFER[slot]]
                for i in range(NT):
                    last = nc.tensor.transpose(ps_turn[:, c % 2, i * P:(i + 1) * P], p[:, i, c * P:(c + 1) * P], ident[:, :])
                last.then_inc(turned, 1)

            def attend(t, slot, c, head):
                n = unit_no(t, slot)
                if c == 0:
                    wait(pe, elu_ready, n - 1)
                    if head is None:
                        pe.wait_ge(acc_lo, t)
                    else:
                        step_, use = (t - 1, f"value{head}") if head in (1,) else (t, f"value{head}")
                        pe.wait_ge(gen_evacuated, GEN_EVAC.after(step_, use))
                pe.wait_ge(turned_lo, 4 * (n - 1) + c + 1)
                v = value_out if head is None else value[:, head % 2]
                for o in range(FT):
                    last = split3(ps_z[:, o, :],
                                  halves(lambda s: v[:, s, c, o * P:(o + 1) * P]),
                                  halves(lambda s: probT[:, c % 2, s, :]), c == 0, c == NT - 1)
                last.then_inc(chunk_used, 1)

            def values(t, use, head):
                gen_claim(t, use)
                pe.wait_ge(gen_evacuated, GEN_EVAC.after(t if head == 0 or head == 1 else t - 1, "h0T"))
                for j in range(NT):
                    for k in range(FT):
                        last = split3(gen_rows[:, j, :], halves(lambda s: h0T[:, s, k, j * P:(j + 1) * P]),
                                      halves(lambda s: W_hl[:, s, k, head * O:(head + 1) * O]), k == 0, k == FT - 1)
                last.then_inc(gen_ready, 1)

            def out_project(b, head):
                if head == 0:
                    wait(pe, acc_lo, b)
                    wait(pe, fout_ready, b)
                pe.wait_ge(z_lo, UNIT_Z(b, head))
                for j in range(NT):
                    for k in range(FT):
                        last = split3(ps_acc[:, j, :],
                                      halves(lambda s: zT[:, head % 2, s, k * N + j * P:k * N + (j + 1) * P]),
                                      halves(lambda s: Wout_hl[:, s, head * FT + k, :]),
                                      head == 0 and k == 0 and j % 2 == 0, head == H - 1 and k == FT - 1,
                                      skip_group_check=True)
                last.then_inc(acc_used, 1)

            def UNIT_Z(b, head):
                return unit_no(b - 1, 4) if head == 0 else unit_no(b, {1: 0, 2: 1, 3: 3}[head])

            def turn_h0(t):
                gen_claim(t, "h0T")
                pe.wait_ge(h0_ready, 4 * (t + 2))
                for k in range(FT):
                    for i in range(NT):
                        last = nc.tensor.transpose(ps_gen[:, k, i * P:(i + 1) * P], xin[:, i, k * P:(k + 1) * P], ident[:, :])
                last.then_inc(gen_ready, 1)

            def f_rows(t):
                gen_claim(t, "frows")
                for k in range(FT):
                    last = split3(ps_gen[0:2 * H, 0, :], halves(lambda s: wa_hl[:, s, k, :]),
                                  halves(lambda s: h0T[:, s, k, :]), k == 0, k == FT - 1)
                last.then_inc(gen_ready, 1)

            def broadcast(t, use, head):
                gen_claim(t, use)
                if head == 0:
                    pe.wait_ge(frow_ready, t + 2)
                last = mm(bcast, select[:, head, :], frow_hl[:, :], start=True, stop=True)
                if head == 0:
                    for i in range(NT):
                        last = nc.tensor.transpose(ps_gen[:, 0, i * 2 * H:(i + 1) * 2 * H], frow[:, i * P:(i + 1) * P],
                                                   ident[0:2 * H, 0:2 * H])
                last.then_inc(gen_ready, 1)

            def broadcast_out(t):
                gen_claim(t, "bcast_out")
                pe.wait_ge(fdiag_ready, 4 * t)
                for j in range(NT):
                    last = mm(bcast[:, j * P:(j + 1) * P], ones[:, :], f2_diag[:, j, :], start=True, stop=True)
                last.then_inc(gen_ready, 1)

            def ffn1(t):
                gen_claim(t, "ffn1")
                pe.wait_ge(z_lo, unit_no(t, 2))
                for m in range(FT):
                    for k in range(FT):
                        last = split3(ps_gen[:, m, :], halves(lambda s: w1_hl[:, s, k, m * P:(m + 1) * P]),
                                      halves(lambda s: oT[:, s, k * N:(k + 1) * N]), k == 0, k == FT - 1)
                last.then_inc(gen_ready, 1)

            def ffn2(t):
                gen_claim(t, "ffn2")
                for i in range(NT):
                    first = i % 2 == 0
                    for k in range(FT):
                        split3(gen_rows[:, i, :], halves(lambda s: rT[:, s, k * N + i * P:k * N + (i + 1) * P]),
                               halves(lambda s: w2_hl[:, s, k, :]), first and k == 0, False, skip_group_check=True)
                    for k in range(FT):
                        for s in range(2):
                            last = mm(gen_rows[:, i, k * P:(k + 1) * P], oT[:, s, k * N + i * P:k * N + (i + 1) * P],
                                      ident_r[:, :], start=False, stop=(s == 1 and k == FT - 1), skip_group_check=True)
                last.then_inc(gen_ready, 1)

            def adj_h(t):
                gen_claim(t, "AH")
                pe.wait_ge(h1_lo, t - 1)
                for d in range(FT):
                    for j in range(NT):
                        for s in (1, 0):
                            last = mm(ps_gen[:, d, :], h1[:, s, j, d * P:(d + 1) * P], adjT[:, j, :],
                                      start=(j == 0 and s == 1), stop=(j == NT - 1 and s == 0))
                last.then_inc(gen_ready, 1)

            def deg_h(t):
                gen_claim(t, "DH")
                for d in range(FT):
                    for j in range(NT):
                        for s in (1, 0):
                            last = mm(ps_gen[:, d, j * P:(j + 1) * P], h1[:, s, j, d * P:(d + 1) * P], deg_diag[:, j, :],
                                      start=(s == 1), stop=(s == 0))
                last.then_inc(gen_ready, 1)

            def layer1(t):
                gen_claim(t, "L1")
                for i in range(NT):
                    for m, src in ((1, rT), (0, dhT)):
                        for k in range(FT):
                            last = split3(gen_rows[:, i, :], halves(lambda s: src[:, s, k * N + i * P:k * N + (i + 1) * P]),
                                          halves(lambda s: wij_hl[:, s, m, k, :]), m == 1 and k == 0, m == 0 and k == FT - 1)
                last.then_inc(gen_ready, 1)

            def unit(t, slot, before=(), middle=(), after=()):
                here = has_unit(t, slot)
                head = HEAD_OF[slot]
                if here:
                    turn(t, slot, 0)
                    turn(t, slot, 1)
                for f in before:
                    f()
                if here:
                    attend(t, slot, 0, head)
                    turn(t, slot, 2)
                    attend(t, slot, 1, head)
                for f in middle:
                    f()
                if here:
                    turn(t, slot, 3)
                    attend(t, slot, 2, head)
                    attend(t, slot, 3, head)
                for f in after:
                    f()

            def step(t):
                A, Bb, C, D = (exists(t, o) for o in (1, 0, -1, -2))
                if isinstance(t, int) and t == FIRST_STEP:
                    pe.wait_ge(halves_lo, HALVES)
                    pe.wait_ge(halves_hi, HALVES)
                    pe.wait_ge(exact_ready, NT + 2)
                    pe.wait_ge(deg_ready, 2)
                unit(t, 0,
                     before=[lambda: values(t, "value2", 2)] * Bb,
                     middle=[lambda: ffn2(t)] * D,
                     after=[lambda: broadcast_out(t)] * C)
                unit(t, 1,
                     before=[lambda: values(t, "value3", 3), lambda: out_project(t, 0)] * Bb,
                     middle=[lambda: turn_h0(t)] * A,
                     after=[lambda: broadcast(t, "bcast3", 3)] * Bb)
                unit(t, 2,
                     before=[lambda: out_project(t, 1)] * Bb + [lambda: f_rows(t)] * A,
                     middle=[lambda: adj_h(t)] * D,
                     after=[lambda: broadcast(t, "bcast0", 0)] * A)
                unit(t, 3,
                     before=[lambda: values(t, "value0", 0)] * A + [lambda: out_project(t, 2)] * Bb + [lambda: deg_h(t)] * D,
                     middle=[lambda: layer1(t)] * D,
                     after=[lambda: broadcast(t, "bcast1", 1)] * A)
                unit(t, 4,
                     before=[lambda: values(t, "value1", 1)] * A,
                     middle=[lambda: ffn1(t)] * C,
                     after=[lambda: out_project(t, 3)] * Bb + [lambda: broadcast(t, "bcast2", 2)] * A)

            steps(pe, step)

        @block.scalar
        def _(act):
            def copy(dst, src):
                return nc.scalar.activation(dst, src, ACT.Copy)

            for i, (dst, src, sem_, value_) in enumerate(SPLITS):
                act.wait_ge(sem_, value_)
                copy(dst[0], src).then_inc(halves_hi, 1)
                if i == 3:
                    for j in range(NT):
                        act.wait_ge(adj_turned, j + 1)
                        copy(adjT[:, j, :], (ps_turn, ps_z)[j // 2][:, j % 2, :]).then_inc(exact_ready, 1)
                    act.wait_ge(ident_ready, 1)
                    copy(ident_r[:, :], ident[:, :]).then_inc(exact_ready, 1)
                    act.wait_ge(const_ready, CONSTS)
                    copy(select[:, :, :], selectf).then_inc(exact_ready, 1)

            def gen_hi_copy(t, use, dst, src):
                act.wait_ge(gen_ready, GEN.after(t, use))
                copy(dst, src).then_inc(gen_hi, 1)

            def value_hi(t, use, head):
                gen_hi_copy(t, use, value[:, head % 2, 0, :, :].rearrange("p n o -> p (n o)"), gen_flat)

            def logits(t, slot):
                n = unit_no(t, slot)
                s = slot % SLOTS
                st = t if slot < SLOTS else t + 1
                use, step_ = (("bcast1", st - 1), ("bcast2", st - 1), ("bcast_out", st), ("bcast3", st), ("bcast0", st))[s]
                act.wait_ge(gen_ready, GEN.after(step_, use))
                head = (1, 2, None, 3, 0)[s]
                if head == 0:
                    copy(f1[:, :, :].rearrange("p n c -> p (n c)"), ps_gen[:, 0, 0:NT * 2 * H]).then_inc(f1_ready, 1)
                    act.wait_ge(f1_ready, st + 2)
                back = {0: 3, 1: 3, 2: 2, 3: 2, 4: 5}[s]
                wait(act, turned, 4 * (n - back) if not isinstance(n, int) else 4 * score_last(st, s))
                for i in range(NT):
                    bias = f_out[:, 0, i:i + 1] if head is None else f1[:, i, head:head + 1]
                    last = nc.scalar.activation(score[SCORE_BUFFER[s]][:, i, :], bcast, ACT.Identity, bias=bias)
                    last.then_inc(logits_ready, 1)

            def score_last(st, s):
                t_, s_ = st, s - 1
                while t_ >= FIRST_STEP:
                    while s_ >= 0:
                        if SCORE_BUFFER[s_] == SCORE_BUFFER[s] and has_unit(t_, s_):
                            return unit_no(t_, s_)
                        s_ -= 1
                    t_, s_ = t_ - 1, SLOTS - 1
                return 0

            def exps(t, slot):
                n = unit_no(t, slot)
                s = slot % SLOTS
                act.wait_ge(negmax_ready, n)
                for i in range(NT):
                    p = score[SCORE_BUFFER[s]][:, i, :]
                    nc.scalar.activation(p, p, ACT.Exp, bias=negmax[:, s, i:i + 1],
                                         accum_out=rowsum[:, s, i:i + 1]).then_inc(exp_done, 1)

            def turned_hi_copy(t, slot, c):
                k = 4 * (unit_no(t, slot) - 1) + c
                act.wait_ge(turned, k + 1)
                wait(act, chunk_used, k - 1)
                copy(probT[:, c % 2, 0, :], ps_turn[:, c % 2, :]).then_inc(turned_hi, 1)

            def elu_first(t, slot):
                n = unit_no(t, slot)
                act.wait_ge(chunk_used, 4 * n)
                wait(act, z_lo, n - 1)
                nc.scalar.activation(elu[:, :], ps_z[:, :, :].rearrange("p a b -> p (a b)"), ACT.Relu,
                                     scale=-1.0).then_inc(z_relu, 1)
                act.wait_ge(z_relu, n)
                nc.scalar.activation(elu[:, :], elu[:, :], ACT.Exp, scale=-1.0).then_inc(z_exp, 1)

            def elu_hi(t, slot):
                n = unit_no(t, slot)
                s = slot % SLOTS
                head = (1, 2, None, 3, 0)[s]
                act.wait_ge(elu_ready, n)
                if head is None:
                    wait(act, gen_ready, GEN.after(t, "ffn2") if exists(t, -2) else 0)
                    copy(oT[:, 0, :], elu[:, :]).then_inc(z_hi, 1)
                else:
                    b = t if slot >= 0 else t
                    wait(act, acc_used, 4 * b + head - 1)
                    copy(zT[:, head % 2, 0, :], elu[:, :]).then_inc(z_hi, 1)

            def acc_hi_copy(t):
                act.wait_ge(acc_used, 4 * t)
                wait(act, chunk_used, 4 * unit_no(t - 1, 2) if exists(t, -2) else 0)
                copy(value_out[:, 0, :, :], ps_acc[:, :, :]).then_inc(acc_hi, 1)

            def h0_relu(t):
                act.wait_ge(nmr_ready[0], t + 2)
                for i in range(NT):
                    nc.scalar.activation(xin[:, i, :], xin[:, i, :], ACT.Relu, bias=nmr[:, 0, i:i + 1],
                                         scale=rstd[:, 0, i:i + 1]).then_inc(h0_ready, 1)

            def h1_relu(t):
                act.wait_ge(nmr_ready[2], t - 1)
                wait(act, st_out, 16 * (t - 2))
                for i in range(NT):
                    last = nc.scalar.activation(h1f[:, i, :], y[:, i, :], ACT.Relu, bias=nmr[:, 2, i:i + 1],
                                                scale=rstd[:, 2, i:i + 1])
                    last.then_inc(h1_ready, 1)
                act.wait_ge(h1_ready, 4 * (t - 1))
                copy(h1[:, 0, :, :], h1f[:, :, :]).then_inc(h1_hi, 1)

            def frow_copy(t):
                act.wait_ge(gen_ready, GEN.after(t, "frows"))
                copy(frow_hl[0:2 * H, :], ps_gen[0:2 * H, 0, :]).then_inc(gen_hi, 1)
                copy(frow[:, :], ps_gen[0:2 * H, 0, :]).then_inc(frow_ready, 1)

            def ffn_relu(t):
                act.wait_ge(gen_ready, GEN.after(t, "ffn1"))
                for m in range(FT):
                    nc.scalar.activation(rF[:, m * N:(m + 1) * N], ps_gen[:, m, :], ACT.Relu,
                                         bias=b1_col[:, m:m + 1]).then_inc(relu_ready, 1)
                act.wait_ge(relu_ready, 2 * t)
                copy(rT[:, 0, :], rF[:, :]).then_inc(gen_hi, 1)

            def step(t):
                A, Bb, C, D = (exists(t, o) for o in (1, 0, -1, -2))

                def slot(s, early=(), late=()):
                    prev = has_unit(t, s - 1)
                    if prev:
                        elu_first(t, s - 1)
                    if has_unit(t, s):
                        turned_hi_copy(t, s, 0)
                        turned_hi_copy(t, s, 1)
                    if prev:
                        elu_hi(t if s else t, s - 1)
                    if has_unit(t, s + 1):
                        logits(t, s + 1)
                    for f in early:
                        f()
                    if has_unit(t, s):
                        turned_hi_copy(t, s, 2)
                    if has_unit(t, s + 1):
                        exps(t, s + 1)
                    for f in late:
                        f()
                    if has_unit(t, s):
                        turned_hi_copy(t, s, 3)

                slot(0, early=[lambda: acc_hi_copy(t)] * C + [lambda: value_hi(t, "value2", 2)] * Bb,
                     late=[lambda: h0_relu(t)] * A)
                slot(1, early=[lambda: value_hi(t, "value3", 3)] * Bb,
                     late=[lambda: gen_hi_copy(t, "h0T", h0T[:, 0, :, :], ps_gen[:, :, :])] * A)
                slot(2, early=[lambda: frow_copy(t)] * A + [lambda: h1_relu(t)] * D,
                     late=[lambda: gen_hi_copy(t, "AH", rT[:, 0, :], gen_flat)] * D)
                slot(3, early=[lambda: value_hi(t, "value0", 0)] * A + [lambda: gen_hi_copy(t, "DH", dhT[:, 0, :], gen_flat)] * D)
                slot(4, early=[lambda: value_hi(t, "value1", 1)] * A, late=[lambda: ffn_relu(t)] * C)

            steps(act, step)

        @block.vector
        def _(dve):
            tt, ts, stt = nc.vector.tensor_tensor, nc.vector.tensor_scalar, nc.vector.scalar_tensor_tensor
            ttr = nc.vector.tensor_tensor_reduce

            def lo(dst, v, hi):
                return tt(dst, v, hi.bitcast(F32), ALU.subtract)

            dve.wait_ge(ld_adj, 16)
            nc.vector.tensor_copy(score[2][:, :, :], score[2][:, :, :].bitcast(I32)).then_inc(adj_float, 1)
            dve.wait_ge(adj_float, 1)
            ts(mask[:, :, :], score[2][:, :, :], 0.0, MASKED, ALU.is_le, ALU.mult).then_inc(mask_ready, 1)
            nc.vector.reduce_sum(deg[:, :], score[2][:, :, :], AX_X).then_inc(deg_ready, 1)
            dve.wait_ge(ident_ready, 1)
            dve.wait_ge(deg_ready, 1)
            for i in range(NT):
                last = ts(deg_diag[:, i, :], ident[:, :], deg[:, i:i + 1], None, ALU.mult)
            last.then_inc(deg_ready, 1)
            dve.wait_ge(ld_W, 16 * FT)
            dve.wait_ge(ld_a, 32)
            n = 0
            for h in range(H):
                a_rows = elu[:, :] if h < 2 else flat(h1f[:, :, :])
                for k in range(FT):
                    for a in range(2):
                        at = (h % 2) * 2 * O + a * O
                        wait(dve, wa_ready, n - 1)
                        ttr(out=scratch[:, n % 2, :], in0=flat(score[0][:, :, :])[:, (k * H + h) * O:(k * H + h + 1) * O],
                            in1=a_rows[:, at:at + O], scale=1.0, scalar=0.0, op0=ALU.mult, op1=ALU.add,
                            accum_out=wa[:, k, a * H + h:a * H + h + 1]).then_inc(wa_ready, 1)
                        n += 1
            for i, (dst, src, sem_, value_) in enumerate(SPLITS):
                dve.wait_ge(sem_, value_)
                dve.wait_ge(halves_hi, i + 1)
                lo(dst[1], src, dst[0]).then_inc(halves_lo, 1)

            def layer_norm(k, m, src_tiles):
                for i in range(NT):
                    nc.vector.bn_stats(bn[:, k, i, :], src_tiles[:, i, :]).then_inc(stats[k], 1)
                wait_apart(dve, stats[k], 8 * (m - 1) + 4, ident_ready)
                for i in range(NT):
                    nc.vector.bn_aggr(mv[:, k, i, :], bn[:, k, i, :]).then_inc(stats[k], 1)
                dve.wait_ge(stats[k], 8 * m)
                ts(veps[:, k, :], mv[:, k, :, 1], EPS, None, ALU.add).then_inc(veps_ready[k], 1)

            def negate_mean(k, m):
                dve.wait_ge(rstd_ready[k], m)
                stt(out=nmr[:, k, :], in0=mv[:, k, :, 0], scalar=-1.0, in1=rstd[:, k, :], op0=ALU.mult,
                    op1=ALU.mult).then_inc(nmr_ready[k], 1)

            def gen_lo(t, use, dst, src, hi):
                dve.wait_ge(gen_ready, GEN.after(t, use))
                dve.wait_ge(gen_hi, GEN_HI.after(t, use))
                lo(dst, src, hi).then_inc(gen_evacuated, 1)

            def value_lo(t, use, head):
                v = value[:, head % 2]
                gen_lo(t, use, flat(v[:, 1, :, :]), gen_flat, flat(v[:, 0, :, :]))

            def softmax_logits(t, slot):
                n, s = unit_no(t, slot), slot % SLOTS
                tile = score[SCORE_BUFFER[s]]

                def leaky(i):
                    dve.wait_ge(logits_ready, 4 * (n - 1) + i + 1)
                    stt(out=tile[:, i, :], in0=tile[:, i, :], scalar=SLOPE, in1=tile[:, i, :], op0=ALU.mult,
                        op1=ALU.max).then_inc(leaky_ready, 1)

                def masked(i):
                    wait_apart(dve, leaky_ready, 4 * (n - 1) + i + 1, ident_ready)
                    ttr(out=tile[:, i, :], in0=tile[:, i, :], in1=mask[:, i, :], scale=1.0, scalar=LOWEST,
                        op0=ALU.add, op1=ALU.max, accum_out=rowmax[:, s, i:i + 1]).then_inc(masked_ready, 1)

                leaky(0)
                for i in range(1, NT):
                    leaky(i)
                    masked(i - 1)
                masked(NT - 1)
                dve.wait_ge(masked_ready, 4 * n)
                ts(negmax[:, s, :], rowmax[:, s, :], -1.0, None, ALU.mult).then_inc(negmax_ready, 1)

            def row_inverse(t, slot):
                n, s = unit_no(t, slot), slot % SLOTS
                dve.wait_ge(exp_done, 4 * n)
                nc.vector.reciprocal(rinv[:, s, :], rowsum[:, s, :]).then_inc(rinv_ready, 1)

            def turned_lo_copy(t, slot, c):
                k = 4 * (unit_no(t, slot) - 1) + c
                dve.wait_ge(turned_hi, k + 1)
                lo(probT[:, c % 2, 1, :], ps_turn[:, c % 2, :], probT[:, c % 2, 0, :]).then_inc(turned_lo, 1)

            def elu_last(t, slot):
                n = unit_no(t, slot)
                dve.wait_ge(z_exp, n)
                stt(out=elu[:, :], in0=elu[:, :], scalar=-1.0, in1=flat(ps_z[:, :, :]), op0=ALU.add,
                    op1=ALU.max).then_inc(elu_ready, 1)

            def elu_lo(t, slot):
                n = unit_no(t, slot)
                head = HEAD_OF[slot % SLOTS]
                dst = oT if head is None else zT[:, head % 2]
                dve.wait_ge(z_hi, n)
                lo(dst[:, 1, :], elu[:, :], dst[:, 0, :]).then_inc(z_lo, 1)

            def acc_evacuate(t):
                dve.wait_ge(acc_hi, t)
                lo(value_out[:, 1, :, :], ps_acc[:, :, :], value_out[:, 0, :, :]).then_inc(acc_lo, 1)
                if exists(t, -2):
                    dve.wait_ge(logits_ready, 4 * unit_no(t - 1, 2))
                for n in range(2 * NT):
                    a, j = n // NT, n % NT
                    wait(dve, fout_ready, 8 * (t - 1) + n - 1)
                    ttr(out=scratch[:, n % 2, :], in0=ps_acc[:, j, :], in1=aout_row[:, a, :], scale=1.0, scalar=0.0,
                        op0=ALU.mult, op1=ALU.add, accum_out=f_out[:, a, j:j + 1]).then_inc(fout_ready, 1)
                dve.wait_ge(fout_ready, 8 * t)
                if exists(t, -2):
                    dve.wait_ge(gen_ready, GEN.after(t - 1, "bcast_out"))
                for j in range(NT):
                    ts(f2_diag[:, j, :], ident[:, :], f_out[:, 1, j:j + 1], None, ALU.mult).then_inc(fdiag_ready, 1)

            def h0_stats(t):
                dve.wait_ge(ld_x, 16 * (t + 2))
                layer_norm(0, t + 2, xin)

            def y_evacuate(t):
                dve.wait_ge(gen_ready, GEN.after(t, "ffn2"))
                wait(dve, out_ready, t - 2)
                tt(y[:, :, :], gen_rows, b2_row[:, :].unsqueeze(1).broadcast_to((P, NT, O)), ALU.add)\
                    .then_inc(gen_evacuated, 1)
                dve.wait_ge(gen_evacuated, GEN_EVAC.after(t, "ffn2"))
                layer_norm(1, t - 1, y)

            def y_normalise(t):
                dve.wait_ge(rstd_ready[1], t - 1)
                for i in range(NT):
                    ts(y[:, i, :], y[:, i, :], mv[:, 1, i, 0:1], rstd[:, 1, i:i + 1], ALU.subtract, ALU.mult)\
                        .then_inc(ynorm_ready, 1)

            def x1_stats(t):
                dve.wait_ge(x1_ready, t - 1)
                layer_norm(2, t - 1, y)

            def h1_lo_copy(t):
                dve.wait_ge(h1_hi, t - 1)
                lo(h1[:, 1, :, :], h1f[:, :, :], h1[:, 0, :, :]).then_inc(h1_lo, 1)
                for i in range(NT):
                    stt(out=y[:, i, :], in0=bL_row[:, :], scalar=deg[:, i:i + 1], in1=y[:, i, :], op0=ALU.mult,
                        op1=ALU.add).then_inc(x1b_ready, 1)

            def frow_lo(t):
                dve.wait_ge(frow_ready, t + 2)
                gen_lo(t, "frows", frow_hl[32:32 + 2 * H, :], ps_gen[0:2 * H, 0, :], frow_hl[0:2 * H, :])

            def ffn_lo(t):
                gen_lo(t, "ffn1", rT[:, 1, :], rF[:, :], rT[:, 0, :])

            def result(t):
                dve.wait_ge(gen_ready, GEN.after(t, "L1"))
                dve.wait_ge(x1b_ready, 4 * (t - 1))
                dve.wait_ge(h1_lo, t - 1)
                tt(h1f[:, :, :], gen_rows, y[:, :, :], ALU.add).then_inc(out_ready, 1)

            def step(t):
                A, Bb, C, D = (exists(t, o) for o in (1, 0, -1, -2))

                def slot(s, first=(), early=(), late=()):
                    prev = has_unit(t, s - 1)
                    if prev:
                        elu_last(t, s - 1)
                    if has_unit(t, s):
                        turned_lo_copy(t, s, 0)
                        turned_lo_copy(t, s, 1)
                    if prev:
                        elu_lo(t, s - 1)
                    for f in first:
                        f()
                    if has_unit(t, s + 1):
                        softmax_logits(t, s + 1)
                    for f in early:
                        f()
                    if has_unit(t, s):
                        turned_lo_copy(t, s, 2)
                    for f in late:
                        f()
                    if has_unit(t, s):
                        turned_lo_copy(t, s, 3)
                    if has_unit(t, s + 1):
                        row_inverse(t, s + 1)

                slot(0, first=[lambda: acc_evacuate(t)] * C + [lambda: h0_stats(t)] * A,
                     early=[lambda: value_lo(t, "value2", 2)] * Bb + [lambda: negate_mean(0, t + 2)] * A,
                     late=[lambda: y_evacuate(t)] * D)
                slot(1, first=[lambda: y_normalise(t)] * D, early=[lambda: value_lo(t, "value3", 3)] * Bb,
                     late=[lambda: x1_stats(t)] * D
                     + [lambda: gen_lo(t, "h0T", h0T[:, 1, :, :], ps_gen[:, :, :], h0T[:, 0, :, :])] * A)
                slot(2, first=[lambda: negate_mean(2, t - 1)] * D, early=[lambda: frow_lo(t)] * A
                     + [lambda: h1_lo_copy(t)] * D,
                     late=[lambda: gen_lo(t, "AH", rT[:, 1, :], gen_flat, rT[:, 0, :])] * D)
                slot(3, early=[lambda: value_lo(t, "value0", 0)] * A
                     + [lambda: gen_lo(t, "DH", dhT[:, 1, :], gen_flat, dhT[:, 0, :])] * D,
                     late=[lambda: result(t)] * D)
                slot(4, early=[lambda: value_lo(t, "value1", 1)] * A, late=[lambda: ffn_lo(t)] * C)

            steps(dve, step)

        @block.gpsimd
        def _(pool):
            nc.gpsimd.memset(ident[:, :], 0.0).then_inc(zeroed, 1)
            nc.gpsimd.memset(selectf, 0.0).then_inc(zeroed, 1)
            nc.gpsimd.memset(frow_hl[:, :].bitcast(F32), 0.0).then_inc(const_ready, 1)
            nc.gpsimd.memset(ones[:, :], 1.0).then_inc(const_ready, 1)
            nc.gpsimd.memset(minus_half[:, :], -0.5).then_inc(const_ready, 1)
            pool.wait_ge(zeroed, 2)
            nc.gpsimd.affine_select(out=ident[:, :], in_=ident[:, :], compare_op=ALU.not_equal, fill=1.0, base=0,
                                    pattern=[[-1, P]], channel_multiplier=1).then_inc(ident_ready, 1)
            for n, first in enumerate((H, 32 + H)):
                pool.wait_ge(const_ready, 3 + n)
                nc.gpsimd.affine_select(out=selectf, in_=selectf, compare_op=ALU.not_equal, fill=1.0,
                                        base=-first, pattern=[[-1, H], [0, P]], channel_multiplier=1)\
                    .then_inc(const_ready, 1)

            def inverse_std(k, m):
                pool.wait_ge(veps_ready[k], m)
                nc.gpsimd.tensor_tensor(rstd[:, k, :], veps[:, k, :], minus_half[:, :], ALU.pow).then_inc(rstd_ready[k], 1)

            def normalise(t, slot):
                n, s = unit_no(t, slot), slot % SLOTS
                wait_apart(pool, rinv_ready, n, ident_ready)
                for i in range(NT):
                    p = score[SCORE_BUFFER[s]][:, i, :]
                    nc.gpsimd.tensor_scalar(p, p, rinv[:, s, i:i + 1], 1.0, ALU.mult, ALU.mult).then_inc(probs_ready, 1)

            def residual(t):
                rows = lambda v: v[:, :].unsqueeze(1).broadcast_to((P, NT, O))
                pool.wait_ge(ld_small, 16 * SMALL_LOADS)
                pool.wait_ge(ld_xres, 16 * (t - 1))
                nc.gpsimd.tensor_tensor(xres[:, :, :], xres[:, :, :], rows(beta_row), ALU.add).then_inc(xb_ready, 1)
                pool.wait_ge(ynorm_ready, 4 * (t - 1))
                nc.gpsimd.tensor_tensor(y[:, :, :], y[:, :, :], rows(gamma_row), ALU.mult).then_inc(ygamma, 1)
                pool.wait_ge(xb_ready, t - 1)
                pool.wait_ge(ygamma, t - 1)
                nc.gpsimd.tensor_tensor(y[:, :, :], y[:, :, :], xres[:, :, :], ALU.add).then_inc(x1_ready, 1)

            def step(t):
                A, D = exists(t, 1), exists(t, -2)
                if A:
                    inverse_std(0, t + 2)
                if has_unit(t, 1):
                    normalise(t, 1)
                if D:
                    inverse_std(1, t - 1)
                    residual(t)
                if has_unit(t, 2):
                    normalise(t, 2)
                if D:
                    inverse_std(2, t - 1)
                for s in (3, 4, 5):
                    if has_unit(t, s):
                        normalise(t, s)

            steps(pool, step)


_INS = ['x', 'adj', 'L0_gnn_W_heads', 'L0_gnn_a_heads', 'L0_gnn_W_out', 'L0_gnn_a_out', 'L0_gnn_w1', 'L0_gnn_b1',
        'L0_gnn_w2', 'L0_gnn_b2', 'L0_gnn_ln_gamma', 'L0_gnn_ln_beta', 'L1_gnn_W', 'L1_gnn_b']


def kernel(**inputs):
    import numpy as np
    import concourse.bacc as bacc
    from concourse import mybir as mb
    from concourse.bass_utils import run_bass_kernel_spmd

    nc = bacc.Bacc("TRN2", target_bir_lowering=False, num_devices=1)
    arrays, args = {}, []
    for name in _INS:
        a = np.ascontiguousarray(inputs[name])
        arrays[f"in_{name}"] = a
        args.append(nc.dram_tensor(f"in_{name}", a.shape, mb.dt.from_np(a.dtype), kind="ExternalInput").ap())
    out = nc.dram_tensor("out", arrays["in_x"].shape, mb.dt.float32, kind="ExternalOutput").ap()
    build(nc, *args, out)
    r = run_bass_kernel_spmd(nc, [arrays], core_ids=[0])
    return r.results[0]["out"]
```

```python
from contextlib import ExitStack

import concourse.bass as bass
from concourse import mybir

F32 = mybir.dt.float32
F32R = mybir.dt.float32r
BF16 = mybir.dt.bfloat16
I32 = mybir.dt.int32
ALU = mybir.AluOpType
ACT = mybir.ActivationFunctionType
AX_X = mybir.AxisListType.X

P = 128
EPS = 1e-5
SLOPE = 0.01
MASKED = -1e30
LOWEST = -3e38
SLOTS = 5
SCORE_BUFFER = (0, 1, 0, 1, 2)

GEN_USES = {
    "ffn2": (-2, False), "value3": (0, True),
    "h0T": (1, True), "frows": (1, True),
    "f1": (1, False), "value0": (1, True), "AH": (-2, True), "DH": (-2, True),
    "L1": (-2, False), "value1": (1, True),
    "ffn1": (-1, True), "value2": (1, True),
}
UNIT_BATCH = (0, 0, -1, 0, 1)
HEAD_OF = (1, 2, None, 3, 0)
OUT_SLOT = 2
FIRST_STEP, LOOP_FROM = -1, 2


class Tally:

    def __init__(self, offsets, batches):
        self.offsets, self.batches = dict(offsets), batches

    def _has(self, t, name):
        return 0 <= t + self.offsets[name] < self.batches

    def after(self, t, name):
        names = list(self.offsets)
        at = names.index(name) + 1
        if isinstance(t, int):
            before = sum(self._has(s, n) for s in range(FIRST_STEP, t) for n in names)
            return before + sum(self._has(t, n) for n in names[:at])
        before = sum(self._has(s, n) for s in range(FIRST_STEP, LOOP_FROM) for n in names)
        return (t - LOOP_FROM) * len(names) + (before + at)


def build(nc, x, adj, W_heads, a_heads, W_out, a_out, w1, b1, w2, b2, gamma, beta, L1_W, L1_b, out):
    B, N, F = x.shape
    H, _, O = W_heads.shape
    assert F == O == 256 and N == 512 and H == 4
    NT, FT = N // P, F // P
    GEN = Tally({n: o for n, (o, _) in GEN_USES.items()}, B)
    GEN_EVAC = Tally({n: o for n, (o, _) in GEN_USES.items() if n != "L1"}, B)
    GEN_HI = Tally({n: o for n, (o, pair) in GEN_USES.items() if pair}, B)
    UNIT = Tally(enumerate(UNIT_BATCH), B)

    def unit_no(t, slot):
        while slot >= SLOTS:
            t, slot = t + 1, slot - SLOTS
        while slot < 0:
            t, slot = t - 1, slot + SLOTS
        return UNIT.after(t, slot)

    def exists(t, offset):
        return not isinstance(t, int) or 0 <= t + offset < B

    def has_unit(t, slot):
        while slot >= SLOTS:
            t, slot = t + 1, slot - SLOTS
        while slot < 0:
            t, slot = t - 1, slot + SLOTS
        return exists(t, UNIT_BATCH[slot])

    def wait(eng, sem, value):
        if not isinstance(value, int) or value > 0:
            eng.wait_ge(sem, value)

    def wait_apart(eng, sem, value, reached):
        if not isinstance(value, int):
            eng.compute_val(value)
        eng.wait_ge(reached, 1)
        wait(eng, sem, value)

    def steps(eng, step):
        for t in range(FIRST_STEP, LOOP_FROM):
            step(t)
        with eng.Fori(LOOP_FROM, B - 2) as t:
            step(t)
        for t in range(B - 2, B + 2):
            step(t)

    with ExitStack() as ctx:
        def sb(name, shape, dt=F32):
            return ctx.enter_context(nc.sbuf_tensor(name, shape, dt))

        def sem(name):
            return ctx.enter_context(nc.semaphore(name))

        ps_turn = ctx.enter_context(nc.psum_tensor("ps_turn", [P, 2, 512], F32))
        ps_z = ctx.enter_context(nc.psum_tensor("ps_z", [P, FT, 512], F32))
        ps_acc = ctx.enter_context(nc.psum_tensor("ps_acc", [P, NT, O], F32))
        ps_gen = ctx.enter_context(nc.psum_tensor("ps_gen", [P, 2, 512], F32))
        gen_flat = ps_gen[:, :, :].rearrange("p a b -> p (a b)")
        gen_rows = gen_flat.rearrange("p (n o) -> p n o", o=O)
        bcast = ps_turn[:, 0, :]

        W_hl = sb("W_hl", [P, 2, FT, H * O], F32R)
        Wout_hl = sb("Wout_hl", [P, 2, H * FT, O], F32R)
        w1_hl = sb("w1_hl", [P, 2, FT, O], F32R)
        w2_hl = sb("w2_hl", [P, 2, FT, O], F32R)
        wij_hl = sb("wij_hl", [P, 2, 2, FT, O], F32R)
        wa_hl = sb("wa_hl", [P, 2, FT, 2 * H], F32R)
        wa = sb("wa", [P, FT, 2 * H])
        adjT = sb("adjT", [P, NT, N], F32R)
        mask = sb("mask", [P, NT, N], BF16)
        deg = sb("deg", [P, NT])
        deg_diag = sb("deg_diag", [P, NT, P], F32R)
        select = sb("select", [40, H, P], F32R)
        ident = sb("ident", [P, P])
        ident_r = sb("ident_r", [P, P], F32R)
        ones = sb("ones", [P, P])
        b1_col = sb("b1_col", [P, FT])
        b2_row = sb("b2_row", [P, O])
        gamma_row = sb("gamma_row", [P, O])
        beta_row = sb("beta_row", [P, O])
        bL_row = sb("bL_row", [P, O])
        aout_row = sb("aout_row", [P, 2, O])
        minus_half = sb("minus_half", [P, NT])

        xin = sb("xin", [P, NT, F])
        h0T = sb("h0T", [P, 2, FT, N], F32R)
        frow = sb("frow", [2 * H, N])
        frow_hl = sb("frow_hl", [40, N], F32R)
        f1 = sb("f1", [P, NT, 2 * H])
        value = sb("value", [P, 2, 2, NT, O], F32R)
        value_out = sb("value_out", [P, 2, NT, O], F32R)
        f_out = sb("f_out", [P, 2, NT])
        f2_diag = sb("f2_diag", [P, NT, P])
        selectf = f2_diag[0:40, :, :]
        scratch = sb("scratch", [P, 2, O])

        score = [sb(f"score{i}", [P, NT, N]) for i in range(3)]
        rowmax = sb("rowmax", [P, SLOTS, NT])
        negmax = sb("negmax", [P, SLOTS, NT])
        rowsum = sb("rowsum", [P, SLOTS, NT])
        rinv = sb("rinv", [P, SLOTS, NT])
        probT = sb("probT", [P, 2, 2, N], F32R)
        elu = sb("elu", [P, FT * N])
        zT = sb("zT", [P, 2, 2, FT * N], F32R)
        oT = sb("oT", [P, 2, FT * N], F32R)

        rT = sb("rT", [P, 2, FT * N], F32R)
        dhT = value_out[:, :, :, :].rearrange("p s n o -> p s (n o)")
        y = sb("y", [P, NT, O])
        xres = sb("xres", [P, NT, F])
        rF = xres[:, :, :].rearrange("p n f -> p (n f)")
        h1f = sb("h1f", [P, NT, O])
        h1 = sb("h1", [P, 2, NT, O], F32R)
        bn = sb("bn", [P, 3, NT, 6])
        mv = sb("mv", [P, 3, NT, 2])
        veps = sb("veps", [P, 3, NT])
        rstd = sb("rstd", [P, 3, NT])
        nmr = sb("nmr", [P, 3, NT])

        ld_x, ld_xres, st_out = sem("ld_x"), sem("ld_xres"), sem("st_out")
        ld_W, ld_a, ld_adj, ld_Wout, ld_L1, ld_small = (
            sem("ld_W"), sem("ld_a"), sem("ld_adj"), sem("ld_Wout"), sem("ld_L1"), sem("ld_small"))
        SMALL_LOADS, CONSTS = 8, 5
        zeroed, ident_ready, const_ready = sem("zeroed"), sem("ident_ready"), sem("const_ready")
        adj_float, mask_ready, deg_ready, adj_turned, L1_turned = (
            sem("adj_float"), sem("mask_ready"), sem("deg_ready"), sem("adj_turned"), sem("L1_turned"))
        wa_ready, halves_hi, halves_lo, exact_ready = (
            sem("wa_ready"), sem("halves_hi"), sem("halves_lo"), sem("exact_ready"))
        gen_ready, gen_hi, gen_evacuated = sem("gen_ready"), sem("gen_hi"), sem("gen_evacuated")
        bcast_ready = sem("bcast_ready")
        logits_ready, leaky_ready, masked_ready = sem("logits_ready"), sem("leaky_ready"), sem("masked_ready")
        negmax_ready, exp_done, rinv_ready, probs_ready = (
            sem("negmax_ready"), sem("exp_done"), sem("rinv_ready"), sem("probs_ready"))
        turned, turned_hi, turned_lo, chunk_used = sem("turned"), sem("turned_hi"), sem("turned_lo"), sem("chunk_used")
        z_ready, z_relu, z_exp, elu_ready, z_hi, z_lo = (
            sem("z_ready"), sem("z_relu"), sem("z_exp"), sem("elu_ready"), sem("z_hi"), sem("z_lo"))
        acc_used, acc_hi, acc_lo, fout_ready, fdiag_ready = (
            sem("acc_used"), sem("acc_hi"), sem("acc_lo"), sem("fout_ready"), sem("fdiag_ready"))
        frow_ready = sem("frow_ready")
        stats, veps_ready, rstd_ready, nmr_ready = (
            [sem(f"{n}{i}") for i in range(3)] for n in ("stats", "veps_ready", "rstd_ready", "nmr_ready"))
        h0_ready, relu_ready, y_ready, ynorm_ready, ygamma, x1_ready, xb_ready = (
            sem("h0_ready"), sem("relu_ready"), sem("y_ready"), sem("ynorm_ready"), sem("ygamma"),
            sem("x1_ready"), sem("xb_ready"))
        h1_ready, h1_hi, h1_lo, x1b_ready, out_ready = (
            sem("h1_ready"), sem("h1_hi"), sem("h1_lo"), sem("x1b_ready"), sem("out_ready"))

        x_tiles = x.rearrange("b (n p) f -> b p n f", p=P)
        out_tiles = out.rearrange("b (n p) f -> b p n f", p=P)

        def row(v):
            return v.rearrange("(a n) -> a n", a=1).broadcast_to((P, v.shape[0]))

        def flat(ap):
            return ap.rearrange("p a b -> p (a b)")

        def hl(t, *at):
            return [flat(t[(slice(None), i, *at)]) if not at else flat(t[:, i, at[0], :, :]) for i in range(2)]

        SPLITS = [
            (hl(W_hl), flat(score[0][:, :, :]), ld_W, 16 * FT),
            (hl(Wout_hl), flat(score[1][:, :, :]), ld_Wout, 16),
            (hl(w1_hl), flat(y[:, 0:2, :]), ld_small, 16 * SMALL_LOADS),
            (hl(w2_hl), flat(y[:, 2:4, :]), ld_small, 16 * SMALL_LOADS),
            (hl(wij_hl, 0), ps_gen[:, 0, :], L1_turned, 1),
            (hl(wij_hl, 1), ps_gen[:, 1, :], L1_turned, 1),
            (hl(wa_hl), flat(wa[:, :, :]), wa_ready, 2 * FT * H),
        ]
        HALVES = len(SPLITS)

        block = ctx.enter_context(nc.Block())

        @block.sync
        def _(sp):
            sp.dma_start(xin[:, :, :], x_tiles[0]).then_inc(ld_x, 16)
            for k in range(FT):
                sp.dma_start(flat(score[0][:, :, :])[:, k * H * O:(k + 1) * H * O].rearrange("p (h o) -> p h o", o=O),
                             W_heads[:, k * P:(k + 1) * P, :].rearrange("h p o -> p h o")).then_inc(ld_W, 16)
            sp.dma_start(elu[:, :], row(a_heads[0:2, :].rearrange("h o -> (h o)"))).then_inc(ld_a, 16)
            sp.dma_start(h1f[:, :, :].rearrange("p n o -> p (n o)"),
                         row(a_heads[2:4, :].rearrange("h o -> (h o)"))).then_inc(ld_a, 16)
            sp.dma_start(score[2][:, :, :].bitcast(I32), adj.rearrange("(n p) j -> p n j", p=P)).then_inc(ld_adj, 16)
            sp.dma_start(score[1][:, :, :].rearrange("p a (b o) -> p (a b) o", o=O),
                         W_out.rearrange("(k p) o -> p k o", p=P)).then_inc(ld_Wout, 16)
            sp.dma_start(xres[:, :, :].rearrange("p (c a) o -> p c (a o)", c=FT),
                         L1_W.rearrange("(c p) d -> p c d", p=P)).then_inc(ld_L1, 16)
            sp.dma_start(y[:, 0:2, :], w1.rearrange("(k p) o -> p k o", p=P)).then_inc(ld_small, 16)
            sp.dma_start(y[:, 2:4, :], w2.rearrange("(k p) o -> p k o", p=P)).then_inc(ld_small, 16)
            with nc.allow_non_contiguous_dma(reason="one bias, once"):
                sp.dma_start(b1_col[:, :], b1.rearrange("(k p) -> p k", p=P)).then_inc(ld_small, 16)
            for dst, src in ((b2_row, b2), (gamma_row, gamma), (beta_row, beta), (bL_row, L1_b)):
                sp.dma_start(dst[:, :], row(src)).then_inc(ld_small, 16)
            sp.dma_start(aout_row[:, :, :].rearrange("p a o -> p (a o)"), row(a_out)).then_inc(ld_small, 16)

            def step(t):
                if exists(t, -2):
                    wait(sp, x1_ready, t - 2)
                    sp.wait_ge(gen_evacuated, GEN_EVAC.after(t - 1, "ffn1"))
                    sp.wait_ge(L1_turned, 1)
                    sp.dma_start(xres[:, :, :], x_tiles[t - 2]).then_inc(ld_xres, 16)
                if exists(t, 2):
                    sp.wait_ge(gen_ready, GEN.after(t, "h0T"))
                    sp.dma_start(xin[:, :, :], x_tiles[t + 2]).then_inc(ld_x, 16)
                if exists(t, -2):
                    sp.wait_ge(out_ready, t - 1)
                    sp.dma_start(out_tiles[t - 2], h1f[:, :, :]).then_inc(st_out, 16)

            steps(sp, step)
            sp.wait_ge(st_out, 16 * B)

        @block.tensor
        def _(pe):
            mm = nc.tensor.matmul

            def split3(dst, stat, mov, first, last, **kw):
                mm(dst, stat[1], mov[0], start=first, stop=False, **kw)
                mm(dst, stat[0], mov[1], start=False, stop=False, **kw)
                return mm(dst, stat[0], mov[0], start=False, stop=last, **kw)

            def halves(ap_of):
                return ap_of(0), ap_of(1)

            def gen_claim(t, use, apart=False):
                names = list(GEN_USES)
                s, at = t, names.index(use)
                while True:
                    at -= 1
                    if at < 0:
                        s, at = s - 1, len(names) - 1
                    if isinstance(s, int) and s < FIRST_STEP:
                        return
                    if exists(s, GEN_USES[names[at]][0]):
                        break
                before = names[at]
                if before == "L1":
                    pe.wait_ge(out_ready, s - 1)
                elif apart:
                    wait_apart(pe, gen_evacuated, GEN_EVAC.after(s, before), ident_ready)
                else:
                    pe.wait_ge(gen_evacuated, GEN_EVAC.after(s, before))

            pe.wait_ge(ident_ready, 1)
            pe.wait_ge(adj_float, 1)
            for j in range(NT):
                bank = (ps_turn, ps_z)[j // 2][:, j % 2, :]
                for i in range(NT):
                    last = nc.tensor.transpose(bank[:, i * P:(i + 1) * P], score[2][:, i, j * P:(j + 1) * P], ident[:, :])
                last.then_inc(adj_turned, 1)
            pe.wait_ge(ld_L1, 16)
            lw = xres[:, :, :].rearrange("p (c a) o -> p c (a o)", c=FT)
            for m in range(2):
                for d in range(FT):
                    for c in range(FT):
                        last = nc.tensor.transpose(ps_gen[:, m, d * O + c * P:d * O + (c + 1) * P],
                                                   lw[:, c, m * F + d * P:m * F + (d + 1) * P], ident[:, :])
            last.then_inc(L1_turned, 1)

            def turn(t, slot, c):
                if not has_unit(t, slot):
                    return
                n = unit_no(t, slot)
                if c == 0:
                    pe.wait_ge(probs_ready, 4 * n)
                    if has_unit(t, slot + 1):
                        pe.wait_ge(logits_ready, 4 * (n + 1))
                wait(pe, turned_lo, 4 * (n - 1) + c - 1)
                p = score[SCORE_BUFFER[slot % SLOTS]]
                for i in range(NT):
                    last = nc.tensor.transpose(ps_turn[:, c % 2, i * P:(i + 1) * P], p[:, i, c * P:(c + 1) * P], ident[:, :])
                last.then_inc(turned, 1)

            def attend(t, slot, c):
                if not has_unit(t, slot):
                    return
                n, head = unit_no(t, slot), HEAD_OF[slot]
                if c == 0:
                    wait(pe, elu_ready, n - 1)
                    if head is None:
                        pe.wait_ge(acc_lo, t)
                    else:
                        pe.wait_ge(gen_evacuated, GEN_EVAC.after(t - 1 if head in (1, 2) else t, f"value{head}"))
                pe.wait_ge(turned_lo, 4 * (n - 1) + c + 1)
                v = value_out if head is None else value[:, head % 2]
                for o in range(FT):
                    last = split3(ps_z[:, o, :],
                                  halves(lambda s: v[:, s, c, o * P:(o + 1) * P]),
                                  halves(lambda s: probT[:, c % 2, s, :]), c == 0, c == NT - 1)
                last.then_inc(chunk_used, 1)

            def values(t, head):
                if not exists(t, 0 if head == 3 else 1):
                    return
                gen_claim(t, f"value{head}")
                pe.wait_ge(gen_evacuated, GEN_EVAC.after(t - 1 if head == 3 else t, "h0T"))
                for j in range(NT):
                    for k in range(FT):
                        last = split3(gen_rows[:, j, :], halves(lambda s: h0T[:, s, k, j * P:(j + 1) * P]),
                                      halves(lambda s: W_hl[:, s, k, head * O:(head + 1) * O]), k == 0, k == FT - 1)
                last.then_inc(gen_ready, 1)

            def out_project(t, head):
                if not exists(t, 0):
                    return
                if head == 0:
                    wait(pe, acc_lo, t)
                    wait(pe, fout_ready, 8 * t)
                pe.wait_ge(z_lo, UNIT_Z(t, head))
                for j in range(NT):
                    for k in range(FT):
                        last = split3(ps_acc[:, j, :],
                                      halves(lambda s: zT[:, head % 2, s, k * N + j * P:k * N + (j + 1) * P]),
                                      halves(lambda s: Wout_hl[:, s, head * FT + k, :]),
                                      head == 0 and k == 0 and j % 2 == 0, head == H - 1 and k == FT - 1,
                                      skip_group_check=True)
                last.then_inc(acc_used, 1)

            def UNIT_Z(b, head):
                return unit_no(b - 1, 4) if head == 0 else unit_no(b, {1: 0, 2: 1, 3: 3}[head])

            def turn_h0(t):
                if not exists(t, 1):
                    return
                gen_claim(t, "h0T")
                pe.wait_ge(h0_ready, 4 * (t + 2))
                for k in range(FT):
                    for i in range(NT):
                        last = nc.tensor.transpose(ps_gen[:, k, i * P:(i + 1) * P], xin[:, i, k * P:(k + 1) * P], ident[:, :])
                last.then_inc(gen_ready, 1)

            def f_rows(t):
                if not exists(t, 1):
                    return
                gen_claim(t, "frows")
                for k in range(FT):
                    last = split3(ps_gen[0:2 * H, 0, :], halves(lambda s: wa_hl[:, s, k, :]),
                                  halves(lambda s: h0T[:, s, k, :]), k == 0, k == FT - 1)
                last.then_inc(gen_ready, 1)

            def f1_columns(t):
                if not exists(t, 1):
                    return
                gen_claim(t, "f1", apart=True)
                for i in range(NT):
                    last = nc.tensor.transpose(ps_gen[:, 0, i * 2 * H:(i + 1) * 2 * H], frow[:, i * P:(i + 1) * P],
                                               ident[0:2 * H, 0:2 * H])
                last.then_inc(gen_ready, 1)

            def broadcast(t, slot):
                if not has_unit(t, slot):
                    return
                n = unit_no(t, slot)
                before = unit_no(t, slot - 2)
                if has_unit(t, slot - 2):
                    pe.wait_ge(turned_lo, 4 * before - 1)
                else:
                    wait(pe, turned_lo, 4 * before)
                    wait(pe, logits_ready, 4 * (n - 1))
                head = HEAD_OF[slot % SLOTS]
                if head is None:
                    pe.wait_ge(fdiag_ready, 4 * t)
                    for j in range(NT):
                        last = mm(bcast[:, j * P:(j + 1) * P], ones[:, :], f2_diag[:, j, :], start=True, stop=True)
                else:
                    if head == 0:
                        pe.wait_ge(gen_evacuated, GEN_EVAC.after(t, "frows"))
                    last = mm(bcast, select[:, head, :], frow_hl[:, :], start=True, stop=True)
                last.then_inc(bcast_ready, 1)

            def ffn1(t):
                if not exists(t, -1):
                    return
                gen_claim(t, "ffn1")
                pe.wait_ge(z_lo, unit_no(t, 2))
                for m in range(FT):
                    for k in range(FT):
                        last = split3(ps_gen[:, m, :], halves(lambda s: w1_hl[:, s, k, m * P:(m + 1) * P]),
                                      halves(lambda s: oT[:, s, k * N:(k + 1) * N]), k == 0, k == FT - 1)
                last.then_inc(gen_ready, 1)

            def ffn2(t):
                if not exists(t, -2):
                    return
                gen_claim(t, "ffn2")
                for i in range(NT):
                    first = i % 2 == 0
                    for k in range(FT):
                        split3(gen_rows[:, i, :], halves(lambda s: rT[:, s, k * N + i * P:k * N + (i + 1) * P]),
                               halves(lambda s: w2_hl[:, s, k, :]), first and k == 0, False, skip_group_check=True)
                    for k in range(FT):
                        for s in range(2):
                            last = mm(gen_rows[:, i, k * P:(k + 1) * P], oT[:, s, k * N + i * P:k * N + (i + 1) * P],
                                      ident_r[:, :], start=False, stop=(s == 1 and k == FT - 1), skip_group_check=True)
                last.then_inc(gen_ready, 1)

            def adj_h(t):
                if not exists(t, -2):
                    return
                gen_claim(t, "AH")
                pe.wait_ge(h1_lo, t - 1)
                for d in range(FT):
                    for j in range(NT):
                        for s in (1, 0):
                            last = mm(ps_gen[:, d, :], h1[:, s, j, d * P:(d + 1) * P], adjT[:, j, :],
                                      start=(j == 0 and s == 1), stop=(j == NT - 1 and s == 0))
                last.then_inc(gen_ready, 1)

            def deg_h(t):
                if not exists(t, -2):
                    return
                gen_claim(t, "DH")
                for d in range(FT):
                    for j in range(NT):
                        for s in (1, 0):
                            last = mm(ps_gen[:, d, j * P:(j + 1) * P], h1[:, s, j, d * P:(d + 1) * P], deg_diag[:, j, :],
                                      start=(s == 1), stop=(s == 0))
                last.then_inc(gen_ready, 1)

            def layer1(t):
                if not exists(t, -2):
                    return
                gen_claim(t, "L1")
                for i in range(NT):
                    for m, src in ((1, rT), (0, dhT)):
                        for k in range(FT):
                            last = split3(gen_rows[:, i, :], halves(lambda s: src[:, s, k * N + i * P:k * N + (i + 1) * P]),
                                          halves(lambda s: wij_hl[:, s, m, k, :]), m == 1 and k == 0, m == 0 and k == FT - 1)
                last.then_inc(gen_ready, 1)

            def step(t):
                if isinstance(t, int) and t == FIRST_STEP:
                    pe.wait_ge(halves_lo, HALVES)
                    pe.wait_ge(halves_hi, HALVES)
                    pe.wait_ge(exact_ready, NT + 2)
                    pe.wait_ge(deg_ready, 2)
                attend(t, 0, 0)
                turn(t, 0, 2)
                attend(t, 0, 1)
                turn(t, 0, 3)
                broadcast(t, 2)
                ffn2(t)
                attend(t, 0, 2)
                attend(t, 0, 3)
                turn(t, 1, 0)
                turn(t, 1, 1)
                values(t, 3)
                attend(t, 1, 0)
                turn(t, 1, 2)
                attend(t, 1, 1)
                turn(t, 1, 3)
                out_project(t, 0)
                broadcast(t, 3)
                turn_h0(t)
                attend(t, 1, 2)
                attend(t, 1, 3)
                turn(t, 2, 0)
                turn(t, 2, 1)
                out_project(t, 1)
                f_rows(t)
                attend(t, 2, 0)
                turn(t, 2, 2)
                attend(t, 2, 1)
                turn(t, 2, 3)
                f1_columns(t)
                broadcast(t, 4)
                values(t, 0)
                attend(t, 2, 2)
                attend(t, 2, 3)
                turn(t, 3, 0)
                turn(t, 3, 1)
                adj_h(t)
                out_project(t, 2)
                deg_h(t)
                attend(t, 3, 0)
                turn(t, 3, 2)
                attend(t, 3, 1)
                turn(t, 3, 3)
                layer1(t)
                broadcast(t, 5)
                attend(t, 3, 2)
                attend(t, 3, 3)
                turn(t, 4, 0)
                turn(t, 4, 1)
                values(t, 1)
                attend(t, 4, 0)
                turn(t, 4, 2)
                attend(t, 4, 1)
                turn(t, 4, 3)
                out_project(t, 3)
                broadcast(t, 6)
                ffn1(t)
                attend(t, 4, 2)
                attend(t, 4, 3)
                turn(t, 5, 0)
                turn(t, 5, 1)
                values(t, 2)

            steps(pe, step)

        @block.scalar
        def _(act):
            def copy(dst, src):
                return nc.scalar.activation(dst, src, ACT.Copy)

            for i, (dst, src, sem_, value_) in enumerate(SPLITS):
                act.wait_ge(sem_, value_)
                copy(dst[0], src).then_inc(halves_hi, 1)
                if i == 3:
                    for j in range(NT):
                        act.wait_ge(adj_turned, j + 1)
                        copy(adjT[:, j, :], (ps_turn, ps_z)[j // 2][:, j % 2, :]).then_inc(exact_ready, 1)
                    act.wait_ge(ident_ready, 1)
                    copy(ident_r[:, :], ident[:, :]).then_inc(exact_ready, 1)
                    act.wait_ge(const_ready, CONSTS)
                    copy(select[:, :, :], selectf).then_inc(exact_ready, 1)

            def gen_hi_copy(t, use, dst, src):
                act.wait_ge(gen_ready, GEN.after(t, use))
                copy(dst, src).then_inc(gen_hi, 1)

            def value_hi(t, head):
                if exists(t, 0 if head == 3 else 1):
                    gen_hi_copy(t, f"value{head}", value[:, head % 2, 0, :, :].rearrange("p n o -> p (n o)"), gen_flat)

            def f1_copy(t):
                if exists(t, 1):
                    act.wait_ge(gen_ready, GEN.after(t, "f1"))
                    copy(f1[:, :, :].rearrange("p n c -> p (n c)"), ps_gen[:, 0, 0:NT * 2 * H]).then_inc(gen_evacuated, 1)

            def logits(t, slot, tiles=range(NT)):
                if not has_unit(t, slot):
                    return
                n, s = unit_no(t, slot), slot % SLOTS
                head = HEAD_OF[s]
                if tiles[0] == 0:
                    act.wait_ge(bcast_ready, n)
                    if head == 0:
                        act.wait_ge(gen_evacuated, GEN_EVAC.after(t, "f1"))
                    wait(act, turned, 4 * same_score_before(t, slot))
                for i in tiles:
                    bias = f_out[:, 0, i:i + 1] if head is None else f1[:, i, head:head + 1]
                    nc.scalar.activation(score[SCORE_BUFFER[s]][:, i, :], bcast, ACT.Identity, bias=bias)\
                        .then_inc(logits_ready, 1)

            def same_score_before(t, slot):
                for back in range(1, SLOTS + 1):
                    if SCORE_BUFFER[(slot - back) % SLOTS] == SCORE_BUFFER[slot % SLOTS]:
                        s = slot - back
                        return unit_no(t, s)
                return 0

            def exps(t, slot, tiles=range(NT)):
                if not has_unit(t, slot):
                    return
                n, s = unit_no(t, slot), slot % SLOTS
                if tiles[0] == 0:
                    act.wait_ge(negmax_ready, n)
                for i in tiles:
                    p = score[SCORE_BUFFER[s]][:, i, :]
                    nc.scalar.activation(p, p, ACT.Exp, bias=negmax[:, s, i:i + 1],
                                         accum_out=rowsum[:, s, i:i + 1]).then_inc(exp_done, 1)

            def turned_hi_copy(t, slot, c):
                if not has_unit(t, slot):
                    return
                k = 4 * (unit_no(t, slot) - 1) + c
                act.wait_ge(turned, k + 1)
                wait(act, chunk_used, k - 1)
                copy(probT[:, c % 2, 0, :], ps_turn[:, c % 2, :]).then_inc(turned_hi, 1)

            def elu_relu(t, slot):
                if not has_unit(t, slot):
                    return
                n = unit_no(t, slot)
                act.wait_ge(chunk_used, 4 * n)
                wait(act, z_lo, n - 1)
                nc.scalar.activation(elu[:, :], ps_z[:, :, :].rearrange("p a b -> p (a b)"), ACT.Relu,
                                     scale=-1.0).then_inc(z_relu, 1)

            def elu_exp(t, slot):
                if not has_unit(t, slot):
                    return
                n = unit_no(t, slot)
                act.wait_ge(z_relu, n)
                nc.scalar.activation(elu[:, :], elu[:, :], ACT.Exp, scale=-1.0).then_inc(z_exp, 1)

            def elu_hi(t, slot):
                if not has_unit(t, slot):
                    return
                n, head = unit_no(t, slot), HEAD_OF[slot]
                act.wait_ge(elu_ready, n)
                if head is None:
                    if exists(t, -2):
                        act.wait_ge(gen_ready, GEN.after(t, "ffn2"))
                    copy(oT[:, 0, :], elu[:, :]).then_inc(z_hi, 1)
                else:
                    wait(act, acc_used, 4 * (t + UNIT_BATCH[slot]) + head - 1)
                    copy(zT[:, head % 2, 0, :], elu[:, :]).then_inc(z_hi, 1)

            def acc_hi_copy(t):
                if exists(t, 0):
                    act.wait_ge(acc_used, 4 * (t + 1))
                    copy(value_out[:, 0, :, :], ps_acc[:, :, :]).then_inc(acc_hi, 1)

            def h0_relu(t):
                if not exists(t, 1):
                    return
                act.wait_ge(nmr_ready[0], t + 2)
                for i in range(NT):
                    nc.scalar.activation(xin[:, i, :], xin[:, i, :], ACT.Relu, bias=nmr[:, 0, i:i + 1],
                                         scale=rstd[:, 0, i:i + 1]).then_inc(h0_ready, 1)

            def h1_relu(t):
                if not exists(t, -2):
                    return
                act.wait_ge(nmr_ready[2], t - 1)
                wait(act, st_out, 16 * (t - 2))
                for i in range(NT):
                    last = nc.scalar.activation(h1f[:, i, :], y[:, i, :], ACT.Relu, bias=nmr[:, 2, i:i + 1],
                                                scale=rstd[:, 2, i:i + 1])
                    last.then_inc(h1_ready, 1)
                act.wait_ge(h1_ready, 4 * (t - 1))
                copy(h1[:, 0, :, :], h1f[:, :, :]).then_inc(h1_hi, 1)

            def frow_copy(t):
                if not exists(t, 1):
                    return
                act.wait_ge(gen_ready, GEN.after(t, "frows"))
                copy(frow_hl[0:2 * H, :], ps_gen[0:2 * H, 0, :]).then_inc(gen_hi, 1)
                copy(frow[:, :], ps_gen[0:2 * H, 0, :]).then_inc(frow_ready, 1)

            def ffn_relu(t):
                if not exists(t, -1):
                    return
                act.wait_ge(gen_ready, GEN.after(t, "ffn1"))
                for m in range(FT):
                    nc.scalar.activation(rF[:, m * N:(m + 1) * N], ps_gen[:, m, :], ACT.Relu,
                                         bias=b1_col[:, m:m + 1]).then_inc(relu_ready, 1)
                act.wait_ge(relu_ready, 2 * t)
                copy(rT[:, 0, :], rF[:, :]).then_inc(gen_hi, 1)

            def h0T_hi(t):
                if exists(t, 1):
                    gen_hi_copy(t, "h0T", h0T[:, 0, :, :], ps_gen[:, :, :])

            def AH_hi(t):
                if exists(t, -2):
                    gen_hi_copy(t, "AH", rT[:, 0, :], gen_flat)

            def DH_hi(t):
                if exists(t, -2):
                    gen_hi_copy(t, "DH", dhT[:, 0, :], gen_flat)

            def step(t):
                exps(t, 1, (0, 1))
                turned_hi_copy(t, 0, 2)
                exps(t, 1, (2, 3))
                turned_hi_copy(t, 0, 3)
                logits(t, 2)
                h0_relu(t)
                elu_relu(t, 0)
                turned_hi_copy(t, 1, 0)
                elu_exp(t, 0)
                turned_hi_copy(t, 1, 1)
                elu_hi(t, 0)
                value_hi(t, 3)
                exps(t, 2, (0, 1))
                turned_hi_copy(t, 1, 2)
                exps(t, 2, (2, 3))
                turned_hi_copy(t, 1, 3)
                logits(t, 3)
                h0T_hi(t)
                elu_relu(t, 1)
                turned_hi_copy(t, 2, 0)
                elu_exp(t, 1)
                turned_hi_copy(t, 2, 1)
                elu_hi(t, 1)
                frow_copy(t)
                exps(t, 3, (0, 1))
                turned_hi_copy(t, 2, 2)
                exps(t, 3, (2, 3))
                turned_hi_copy(t, 2, 3)
                f1_copy(t)
                logits(t, 4)
                h1_relu(t)
                value_hi(t, 0)
                elu_relu(t, 2)
                turned_hi_copy(t, 3, 0)
                elu_exp(t, 2)
                turned_hi_copy(t, 3, 1)
                elu_hi(t, 2)
                AH_hi(t)
                DH_hi(t)
                exps(t, 4, (0, 1))
                turned_hi_copy(t, 3, 2)
                exps(t, 4, (2, 3))
                turned_hi_copy(t, 3, 3)
                logits(t, 5)
                elu_relu(t, 3)
                turned_hi_copy(t, 4, 0)
                elu_exp(t, 3)
                turned_hi_copy(t, 4, 1)
                elu_hi(t, 3)
                value_hi(t, 1)
                exps(t, 5, (0, 1))
                turned_hi_copy(t, 4, 2)
                exps(t, 5, (2, 3))
                turned_hi_copy(t, 4, 3)
                logits(t, 6)
                acc_hi_copy(t)
                ffn_relu(t)
                elu_relu(t, 4)
                turned_hi_copy(t, 5, 0)
                elu_exp(t, 4)
                turned_hi_copy(t, 5, 1)
                elu_hi(t, 4)
                value_hi(t, 2)

            steps(act, step)

        @block.vector
        def _(dve):
            tt, ts, stt = nc.vector.tensor_tensor, nc.vector.tensor_scalar, nc.vector.scalar_tensor_tensor
            ttr = nc.vector.tensor_tensor_reduce

            def lo(dst, v, hi):
                return tt(dst, v, hi.bitcast(F32), ALU.subtract)

            dve.wait_ge(ld_adj, 16)
            nc.vector.tensor_copy(score[2][:, :, :], score[2][:, :, :].bitcast(I32)).then_inc(adj_float, 1)
            dve.wait_ge(adj_float, 1)
            ts(mask[:, :, :], score[2][:, :, :], 0.0, MASKED, ALU.is_le, ALU.mult).then_inc(mask_ready, 1)
            nc.vector.reduce_sum(deg[:, :], score[2][:, :, :], AX_X).then_inc(deg_ready, 1)
            dve.wait_ge(ident_ready, 1)
            dve.wait_ge(deg_ready, 1)
            for i in range(NT):
                last = ts(deg_diag[:, i, :], ident[:, :], deg[:, i:i + 1], None, ALU.mult)
            last.then_inc(deg_ready, 1)
            dve.wait_ge(ld_W, 16 * FT)
            dve.wait_ge(ld_a, 32)
            n = 0
            for h in range(H):
                a_rows = elu[:, :] if h < 2 else flat(h1f[:, :, :])
                for k in range(FT):
                    for a in range(2):
                        at = (h % 2) * 2 * O + a * O
                        wait(dve, wa_ready, n - 1)
                        ttr(out=scratch[:, n % 2, :], in0=flat(score[0][:, :, :])[:, (k * H + h) * O:(k * H + h + 1) * O],
                            in1=a_rows[:, at:at + O], scale=1.0, scalar=0.0, op0=ALU.mult, op1=ALU.add,
                            accum_out=wa[:, k, a * H + h:a * H + h + 1]).then_inc(wa_ready, 1)
                        n += 1
            for i, (dst, src, sem_, value_) in enumerate(SPLITS):
                dve.wait_ge(sem_, value_)
                dve.wait_ge(halves_hi, i + 1)
                lo(dst[1], src, dst[0]).then_inc(halves_lo, 1)

            def layer_norm(k, m, src_tiles):
                for i in range(NT):
                    nc.vector.bn_stats(bn[:, k, i, :], src_tiles[:, i, :]).then_inc(stats[k], 1)
                wait_apart(dve, stats[k], 8 * (m - 1) + 4, ident_ready)
                for i in range(NT):
                    nc.vector.bn_aggr(mv[:, k, i, :], bn[:, k, i, :]).then_inc(stats[k], 1)
                dve.wait_ge(stats[k], 8 * m)
                ts(veps[:, k, :], mv[:, k, :, 1], EPS, None, ALU.add).then_inc(veps_ready[k], 1)

            def negate_mean(t, k):
                if not exists(t, 1 if k == 0 else -2):
                    return
                m = t + 2 if k == 0 else t - 1
                dve.wait_ge(rstd_ready[k], m)
                stt(out=nmr[:, k, :], in0=mv[:, k, :, 0], scalar=-1.0, in1=rstd[:, k, :], op0=ALU.mult,
                    op1=ALU.mult).then_inc(nmr_ready[k], 1)

            def gen_lo(t, use, dst, src, hi):
                dve.wait_ge(gen_ready, GEN.after(t, use))
                dve.wait_ge(gen_hi, GEN_HI.after(t, use))
                lo(dst, src, hi).then_inc(gen_evacuated, 1)

            def value_lo(t, head):
                if exists(t, 0 if head == 3 else 1):
                    v = value[:, head % 2]
                    gen_lo(t, f"value{head}", flat(v[:, 1, :, :]), gen_flat, flat(v[:, 0, :, :]))

            def h0T_lo(t):
                if exists(t, 1):
                    gen_lo(t, "h0T", h0T[:, 1, :, :], ps_gen[:, :, :], h0T[:, 0, :, :])

            def AH_lo(t):
                if exists(t, -2):
                    gen_lo(t, "AH", rT[:, 1, :], gen_flat, rT[:, 0, :])

            def DH_lo(t):
                if exists(t, -2):
                    gen_lo(t, "DH", dhT[:, 1, :], gen_flat, dhT[:, 0, :])

            def masks(t, slot, tiles):
                if not has_unit(t, slot):
                    return
                n, s = unit_no(t, slot), slot % SLOTS
                tile = score[SCORE_BUFFER[s]]
                for i in tiles:
                    dve.wait_ge(logits_ready, 4 * (n - 1) + i + 1)
                    stt(out=tile[:, i, :], in0=tile[:, i, :], scalar=SLOPE, in1=tile[:, i, :], op0=ALU.mult,
                        op1=ALU.max).then_inc(leaky_ready, 1)
                for i in tiles:
                    wait_apart(dve, leaky_ready, 4 * (n - 1) + i + 1, ident_ready)
                    ttr(out=tile[:, i, :], in0=tile[:, i, :], in1=mask[:, i, :], scale=1.0, scalar=LOWEST,
                        op0=ALU.add, op1=ALU.max, accum_out=rowmax[:, s, i:i + 1]).then_inc(masked_ready, 1)
                if i == NT - 1:
                    dve.wait_ge(masked_ready, 4 * n)
                    ts(negmax[:, s, :], rowmax[:, s, :], -1.0, None, ALU.mult).then_inc(negmax_ready, 1)

            def row_inverse(t, slot):
                if not has_unit(t, slot):
                    return
                n, s = unit_no(t, slot), slot % SLOTS
                dve.wait_ge(exp_done, 4 * n)
                nc.vector.reciprocal(rinv[:, s, :], rowsum[:, s, :]).then_inc(rinv_ready, 1)

            def turned_lo_copy(t, slot, c):
                if not has_unit(t, slot):
                    return
                k = 4 * (unit_no(t, slot) - 1) + c
                dve.wait_ge(turned_hi, k + 1)
                lo(probT[:, c % 2, 1, :], ps_turn[:, c % 2, :], probT[:, c % 2, 0, :]).then_inc(turned_lo, 1)

            def elu_last(t, slot):
                if not has_unit(t, slot):
                    return
                n = unit_no(t, slot)
                dve.wait_ge(z_exp, n)
                stt(out=elu[:, :], in0=elu[:, :], scalar=-1.0, in1=flat(ps_z[:, :, :]), op0=ALU.add,
                    op1=ALU.max).then_inc(elu_ready, 1)

            def elu_lo(t, slot):
                if not has_unit(t, slot):
                    return
                n, head = unit_no(t, slot), HEAD_OF[slot]
                dst = oT if head is None else zT[:, head % 2]
                dve.wait_ge(z_hi, n)
                lo(dst[:, 1, :], elu[:, :], dst[:, 0, :]).then_inc(z_lo, 1)

            def acc_lo_copy(t):
                if exists(t, 0):
                    dve.wait_ge(acc_hi, t + 1)
                    lo(value_out[:, 1, :, :], ps_acc[:, :, :], value_out[:, 0, :, :]).then_inc(acc_lo, 1)

            def out_logit_parts(t, a):
                if not exists(t, 0):
                    return
                if a == 0:
                    dve.wait_ge(acc_used, 4 * (t + 1))
                    if exists(t, -1):
                        dve.wait_ge(logits_ready, 4 * unit_no(t, OUT_SLOT))
                for j in range(NT):
                    m = 8 * t + 4 * a + j
                    wait(dve, fout_ready, m - 1)
                    ttr(out=scratch[:, j % 2, :], in0=ps_acc[:, j, :], in1=aout_row[:, a, :], scale=1.0, scalar=0.0,
                        op0=ALU.mult, op1=ALU.add, accum_out=f_out[:, a, j:j + 1]).then_inc(fout_ready, 1)

            def h0_stats(t):
                if not exists(t, 1):
                    return
                dve.wait_ge(ld_x, 16 * (t + 2))
                layer_norm(0, t + 2, xin)

            def y_evacuate(t):
                if not exists(t, -2):
                    return
                dve.wait_ge(gen_ready, GEN.after(t, "ffn2"))
                wait(dve, out_ready, t - 2)
                tt(y[:, :, :], gen_rows, b2_row[:, :].unsqueeze(1).broadcast_to((P, NT, O)), ALU.add)\
                    .then_inc(gen_evacuated, 1)
                dve.wait_ge(gen_evacuated, GEN_EVAC.after(t, "ffn2"))
                layer_norm(1, t - 1, y)

            def y_normalise(t):
                if not exists(t, -2):
                    return
                dve.wait_ge(rstd_ready[1], t - 1)
                for i in range(NT):
                    ts(y[:, i, :], y[:, i, :], mv[:, 1, i, 0:1], rstd[:, 1, i:i + 1], ALU.subtract, ALU.mult)\
                        .then_inc(ynorm_ready, 1)

            def x1_stats(t):
                if not exists(t, -2):
                    return
                dve.wait_ge(x1_ready, t - 1)
                layer_norm(2, t - 1, y)

            def h1_lo_copy(t):
                if not exists(t, -2):
                    return
                dve.wait_ge(h1_hi, t - 1)
                lo(h1[:, 1, :, :], h1f[:, :, :], h1[:, 0, :, :]).then_inc(h1_lo, 1)

            def add_bias(t):
                if not exists(t, -2):
                    return
                for i in range(NT):
                    stt(out=y[:, i, :], in0=bL_row[:, :], scalar=deg[:, i:i + 1], in1=y[:, i, :], op0=ALU.mult,
                        op1=ALU.add).then_inc(x1b_ready, 1)

            def frow_lo(t):
                if not exists(t, 1):
                    return
                dve.wait_ge(frow_ready, t + 2)
                gen_lo(t, "frows", frow_hl[32:32 + 2 * H, :], ps_gen[0:2 * H, 0, :], frow_hl[0:2 * H, :])

            def ffn_lo(t):
                if not exists(t, -1):
                    return
                gen_lo(t, "ffn1", rT[:, 1, :], rF[:, :], rT[:, 0, :])

            def result(t):
                if not exists(t, -2):
                    return
                dve.wait_ge(gen_ready, GEN.after(t, "L1"))
                dve.wait_ge(x1b_ready, 4 * (t - 1))
                dve.wait_ge(h1_lo, t - 1)
                tt(h1f[:, :, :], gen_rows, y[:, :, :], ALU.add).then_inc(out_ready, 1)

            def step(t):
                h0_stats(t)
                turned_lo_copy(t, 0, 2)
                turned_lo_copy(t, 0, 3)
                row_inverse(t, 1)
                negate_mean(t, 0)
                masks(t, 2, (0, 1))
                masks(t, 2, (2, 3))
                y_evacuate(t)
                turned_lo_copy(t, 1, 0)
                elu_last(t, 0)
                turned_lo_copy(t, 1, 1)
                elu_lo(t, 0)
                value_lo(t, 3)
                y_normalise(t)
                turned_lo_copy(t, 1, 2)
                turned_lo_copy(t, 1, 3)
                row_inverse(t, 2)
                masks(t, 3, (0, 1))
                masks(t, 3, (2, 3))
                h0T_lo(t)
                turned_lo_copy(t, 2, 0)
                elu_last(t, 1)
                turned_lo_copy(t, 2, 1)
                elu_lo(t, 1)
                x1_stats(t)
                frow_lo(t)
                turned_lo_copy(t, 2, 2)
                turned_lo_copy(t, 2, 3)
                row_inverse(t, 3)
                negate_mean(t, 2)
                masks(t, 4, (0, 1))
                masks(t, 4, (2, 3))
                h1_lo_copy(t)
                value_lo(t, 0)
                turned_lo_copy(t, 3, 0)
                elu_last(t, 2)
                turned_lo_copy(t, 3, 1)
                elu_lo(t, 2)
                AH_lo(t)
                DH_lo(t)
                add_bias(t)
                turned_lo_copy(t, 3, 2)
                turned_lo_copy(t, 3, 3)
                row_inverse(t, 4)
                masks(t, 5, (0, 1))
                masks(t, 5, (2, 3))
                result(t)
                turned_lo_copy(t, 4, 0)
                elu_last(t, 3)
                turned_lo_copy(t, 4, 1)
                elu_lo(t, 3)
                value_lo(t, 1)
                turned_lo_copy(t, 4, 2)
                turned_lo_copy(t, 4, 3)
                row_inverse(t, 5)
                masks(t, 6, (0, 1))
                masks(t, 6, (2, 3))
                acc_lo_copy(t)
                ffn_lo(t)
                turned_lo_copy(t, 5, 0)
                elu_last(t, 4)
                turned_lo_copy(t, 5, 1)
                elu_lo(t, 4)
                out_logit_parts(t, 0)
                out_logit_parts(t, 1)
                value_lo(t, 2)

            steps(dve, step)

        @block.gpsimd
        def _(pool):
            nc.gpsimd.memset(ident[:, :], 0.0).then_inc(zeroed, 1)
            nc.gpsimd.memset(selectf, 0.0).then_inc(zeroed, 1)
            nc.gpsimd.memset(frow_hl[:, :].bitcast(F32), 0.0).then_inc(const_ready, 1)
            nc.gpsimd.memset(ones[:, :], 1.0).then_inc(const_ready, 1)
            nc.gpsimd.memset(minus_half[:, :], -0.5).then_inc(const_ready, 1)
            pool.wait_ge(zeroed, 2)
            nc.gpsimd.affine_select(out=ident[:, :], in_=ident[:, :], compare_op=ALU.not_equal, fill=1.0, base=0,
                                    pattern=[[-1, P]], channel_multiplier=1).then_inc(ident_ready, 1)
            for n, first in enumerate((H, 32 + H)):
                pool.wait_ge(const_ready, 3 + n)
                nc.gpsimd.affine_select(out=selectf, in_=selectf, compare_op=ALU.not_equal, fill=1.0,
                                        base=-first, pattern=[[-1, H], [0, P]], channel_multiplier=1)\
                    .then_inc(const_ready, 1)

            def inverse_std(t, k):
                if not exists(t, 1 if k == 0 else -2):
                    return
                m = t + 2 if k == 0 else t - 1
                pool.wait_ge(veps_ready[k], m)
                nc.gpsimd.tensor_tensor(rstd[:, k, :], veps[:, k, :], minus_half[:, :], ALU.pow).then_inc(rstd_ready[k], 1)

            def normalise(t, slot):
                if not has_unit(t, slot):
                    return
                n, s = unit_no(t, slot), slot % SLOTS
                wait_apart(pool, rinv_ready, n, ident_ready)
                for i in range(NT):
                    p = score[SCORE_BUFFER[s]][:, i, :]
                    nc.gpsimd.tensor_scalar(p, p, rinv[:, s, i:i + 1], 1.0, ALU.mult, ALU.mult).then_inc(probs_ready, 1)

            def rows(v):
                return v[:, :].unsqueeze(1).broadcast_to((P, NT, O))

            def x_beta(t):
                if exists(t, -2):
                    pool.wait_ge(ld_small, 16 * SMALL_LOADS)
                    pool.wait_ge(ld_xres, 16 * (t - 1))
                    nc.gpsimd.tensor_tensor(xres[:, :, :], xres[:, :, :], rows(beta_row), ALU.add).then_inc(xb_ready, 1)

            def y_gamma(t):
                if exists(t, -2):
                    pool.wait_ge(ynorm_ready, 4 * (t - 1))
                    nc.gpsimd.tensor_tensor(y[:, :, :], y[:, :, :], rows(gamma_row), ALU.mult).then_inc(ygamma, 1)

            def x1_sum(t):
                if exists(t, -2):
                    pool.wait_ge(xb_ready, t - 1)
                    pool.wait_ge(ygamma, t - 1)
                    nc.gpsimd.tensor_tensor(y[:, :, :], y[:, :, :], xres[:, :, :], ALU.add).then_inc(x1_ready, 1)

            def out_diagonal(t):
                if not exists(t, 0):
                    return
                if exists(t, -1):
                    pool.wait_ge(bcast_ready, unit_no(t, OUT_SLOT))
                wait_apart(pool, fout_ready, 8 * (t + 1), ident_ready)
                for j in range(NT):
                    nc.gpsimd.tensor_scalar(f2_diag[:, j, :], ident[:, :], f_out[:, 1, j:j + 1], 1.0, ALU.mult,
                                            ALU.mult).then_inc(fdiag_ready, 1)

            def step(t):
                inverse_std(t, 0)
                x_beta(t)
                normalise(t, 1)
                inverse_std(t, 1)
                y_gamma(t)
                normalise(t, 2)
                x1_sum(t)
                inverse_std(t, 2)
                normalise(t, 3)
                normalise(t, 4)
                normalise(t, 5)
                out_diagonal(t)

            steps(pool, step)


_INS = ['x', 'adj', 'L0_gnn_W_heads', 'L0_gnn_a_heads', 'L0_gnn_W_out', 'L0_gnn_a_out', 'L0_gnn_w1', 'L0_gnn_b1',
        'L0_gnn_w2', 'L0_gnn_b2', 'L0_gnn_ln_gamma', 'L0_gnn_ln_beta', 'L1_gnn_W', 'L1_gnn_b']


def kernel(**inputs):
    import numpy as np
    import concourse.bacc as bacc
    from concourse import mybir as mb
    from concourse.bass_utils import run_bass_kernel_spmd

    nc = bacc.Bacc("TRN2", target_bir_lowering=False, num_devices=1)
    arrays, args = {}, []
    for name in _INS:
        a = np.ascontiguousarray(inputs[name])
        arrays[f"in_{name}"] = a
        args.append(nc.dram_tensor(f"in_{name}", a.shape, mb.dt.from_np(a.dtype), kind="ExternalInput").ap())
    out = nc.dram_tensor("out", arrays["in_x"].shape, mb.dt.float32, kind="ExternalOutput").ap()
    build(nc, *args, out)
    r = run_bass_kernel_spmd(nc, [arrays], core_ids=[0])
    return r.results[0]["out"]
```

```python
from contextlib import ExitStack

import concourse.bass as bass
from concourse import mybir

F32 = mybir.dt.float32
F32R = mybir.dt.float32r
BF16 = mybir.dt.bfloat16
I32 = mybir.dt.int32
ALU = mybir.AluOpType
ACT = mybir.ActivationFunctionType
AX_X = mybir.AxisListType.X

P = 128
EPS = 1e-5
SLOPE = 0.01
MASKED = -1e30
LOWEST = -3e38
SLOTS = 5
SCORE_BUFFER = (0, 1, 0, 1, 2)

GEN_USES = {
    "ffn2": (-2, False), "value3": (0, True),
    "h0T": (1, True), "frows": (1, True),
    "f1": (1, False), "value0": (1, True), "AH": (-2, True), "DH": (-2, True),
    "L1": (-2, False), "value1": (1, True),
    "ffn1": (-1, True), "value2": (1, True),
}
UNIT_BATCH = (0, 0, -1, 0, 1)
HEAD_OF = (1, 2, None, 3, 0)
OUT_SLOT = 2
FIRST_STEP, LOOP_FROM = -1, 2


class Tally:

    def __init__(self, offsets, batches):
        self.offsets, self.batches = dict(offsets), batches

    def _has(self, t, name):
        return 0 <= t + self.offsets[name] < self.batches

    def after(self, t, name):
        names = list(self.offsets)
        at = names.index(name) + 1
        if isinstance(t, int):
            before = sum(self._has(s, n) for s in range(FIRST_STEP, t) for n in names)
            return before + sum(self._has(t, n) for n in names[:at])
        before = sum(self._has(s, n) for s in range(FIRST_STEP, LOOP_FROM) for n in names)
        return (t - LOOP_FROM) * len(names) + (before + at)


def build(nc, x, adj, W_heads, a_heads, W_out, a_out, w1, b1, w2, b2, gamma, beta, L1_W, L1_b, out):
    B, N, F = x.shape
    H, _, O = W_heads.shape
    assert F == O == 256 and N == 512 and H == 4
    NT, FT = N // P, F // P
    GEN = Tally({n: o for n, (o, _) in GEN_USES.items()}, B)
    GEN_EVAC = Tally({n: o for n, (o, _) in GEN_USES.items() if n != "L1"}, B)
    GEN_HI = Tally({n: o for n, (o, pair) in GEN_USES.items() if pair}, B)
    UNIT = Tally(enumerate(UNIT_BATCH), B)

    def unit_no(t, slot):
        while slot >= SLOTS:
            t, slot = t + 1, slot - SLOTS
        while slot < 0:
            t, slot = t - 1, slot + SLOTS
        return UNIT.after(t, slot)

    def exists(t, offset):
        return not isinstance(t, int) or 0 <= t + offset < B

    def does_h0(t, ahead):
        return ahead == (isinstance(t, int) and t == FIRST_STEP) and exists(t, 1)

    def has_unit(t, slot):
        while slot >= SLOTS:
            t, slot = t + 1, slot - SLOTS
        while slot < 0:
            t, slot = t - 1, slot + SLOTS
        return exists(t, UNIT_BATCH[slot])

    def wait(eng, sem, value):
        if not isinstance(value, int) or value > 0:
            eng.wait_ge(sem, value)

    def wait_apart(eng, sem, value, reached):
        if not isinstance(value, int):
            eng.compute_val(value)
        eng.wait_ge(reached, 1)
        wait(eng, sem, value)

    def steps(eng, step, drain=None):
        for t in range(FIRST_STEP, LOOP_FROM):
            step(t)
        with eng.Fori(LOOP_FROM, B - 2) as t:
            step(t)
        for t in range(B - 2, B):
            step(t)
        for t in range(B, B + 2):
            (drain or step)(t)

    with ExitStack() as ctx:
        def sb(name, shape, dt=F32):
            return ctx.enter_context(nc.sbuf_tensor(name, shape, dt))

        def sem(name):
            return ctx.enter_context(nc.semaphore(name))

        ps_turn = ctx.enter_context(nc.psum_tensor("ps_turn", [P, 2, 512], F32))
        ps_z = ctx.enter_context(nc.psum_tensor("ps_z", [P, FT, 512], F32))
        ps_acc = ctx.enter_context(nc.psum_tensor("ps_acc", [P, NT, O], F32))
        ps_gen = ctx.enter_context(nc.psum_tensor("ps_gen", [P, 2, 512], F32))
        gen_flat = ps_gen[:, :, :].rearrange("p a b -> p (a b)")
        gen_rows = gen_flat.rearrange("p (n o) -> p n o", o=O)

        def no_heads(t):
            return isinstance(t, int) and t >= B

        def dh_bank(t):
            return ps_acc[:, :, :].rearrange("p n o -> p (n o)") if no_heads(t) else gen_flat

        bcast = ps_turn[:, 0, :]

        W_hl = sb("W_hl", [P, 2, FT, H * O], F32R)
        Wout_hl = sb("Wout_hl", [P, 2, H * FT, O], F32R)
        w1_hl = sb("w1_hl", [P, 2, FT, O], F32R)
        w2_hl = sb("w2_hl", [P, 2, FT, O], F32R)
        wij_hl = sb("wij_hl", [P, 2, 2, FT, O], F32R)
        wa_hl = sb("wa_hl", [P, 2, FT, 2 * H], F32R)
        wa = sb("wa", [P, FT, 2 * H])
        adjT = sb("adjT", [P, NT, N], F32R)
        mask = sb("mask", [P, NT, N], BF16)
        deg = sb("deg", [P, NT])
        deg_diag = sb("deg_diag", [P, NT, P], F32R)
        select = sb("select", [40, H, P], F32R)
        ident = sb("ident", [P, P])
        ident_r = sb("ident_r", [P, P], F32R)
        ones = sb("ones", [P, P])
        b1_col = sb("b1_col", [P, FT])
        b2_row = sb("b2_row", [P, O])
        gamma_row = sb("gamma_row", [P, O])
        beta_row = sb("beta_row", [P, O])
        bL_row = sb("bL_row", [P, O])
        aout_row = sb("aout_row", [P, 2, O])
        minus_half = sb("minus_half", [P, NT])

        xin = sb("xin", [P, NT, F])
        h0T = sb("h0T", [P, 2, FT, N], F32R)
        frow = sb("frow", [2 * H, N])
        frow_hl = sb("frow_hl", [40, N], F32R)
        f1 = sb("f1", [P, NT, 2 * H])
        value = sb("value", [P, 2, 2, NT, O], F32R)
        value_out = sb("value_out", [P, 2, NT, O], F32R)
        f_out = sb("f_out", [P, 2, NT])
        f2_diag = sb("f2_diag", [P, NT, P])
        selectf = f2_diag[0:40, :, :]
        scratch = sb("scratch", [P, 2, O])

        score = [sb(f"score{i}", [P, NT, N]) for i in range(3)]
        rowmax = sb("rowmax", [P, SLOTS, NT])
        negmax = sb("negmax", [P, SLOTS, NT])
        rowsum = sb("rowsum", [P, SLOTS, NT])
        rinv = sb("rinv", [P, SLOTS, NT])
        probT = sb("probT", [P, 2, 2, N], F32R)
        elu = sb("elu", [P, FT * N])
        zT = sb("zT", [P, 2, 2, FT * N], F32R)
        oT = sb("oT", [P, 2, FT * N], F32R)

        rT = sb("rT", [P, 2, FT * N], F32R)
        dhT = value_out[:, :, :, :].rearrange("p s n o -> p s (n o)")
        y = sb("y", [P, NT, O])
        xres = sb("xres", [P, NT, F])
        rF = xres[:, :, :].rearrange("p n f -> p (n f)")
        h1f = sb("h1f", [P, NT, O])
        h1 = sb("h1", [P, 2, NT, O], F32R)
        bn = sb("bn", [P, 3, NT, 6])
        mv = sb("mv", [P, 3, NT, 2])
        veps = sb("veps", [P, 3, NT])
        rstd = sb("rstd", [P, 3, NT])
        nmr = sb("nmr", [P, 3, NT])

        ld_x, ld_xres, st_out = sem("ld_x"), sem("ld_xres"), sem("st_out")
        ld_W, ld_a, ld_adj, ld_Wout, ld_L1, ld_small = (
            sem("ld_W"), sem("ld_a"), sem("ld_adj"), sem("ld_Wout"), sem("ld_L1"), sem("ld_small"))
        SMALL_LOADS, CONSTS = 8, 5
        zeroed, ident_ready, const_ready = sem("zeroed"), sem("ident_ready"), sem("const_ready")
        adj_float, deg_ready, adj_turned, L1_turned = (
            sem("adj_float"), sem("deg_ready"), sem("adj_turned"), sem("L1_turned"))
        wa_ready, halves_hi, halves_lo, exact_ready = (
            sem("wa_ready"), sem("halves_hi"), sem("halves_lo"), sem("exact_ready"))
        gen_ready, gen_hi, gen_evacuated = sem("gen_ready"), sem("gen_hi"), sem("gen_evacuated")
        bcast_ready = sem("bcast_ready")
        logits_ready, leaky_ready, masked_ready = sem("logits_ready"), sem("leaky_ready"), sem("masked_ready")
        negmax_ready, exp_done, rinv_ready, probs_ready = (
            sem("negmax_ready"), sem("exp_done"), sem("rinv_ready"), sem("probs_ready"))
        turned, turned_hi, turned_lo, chunk_used = sem("turned"), sem("turned_hi"), sem("turned_lo"), sem("chunk_used")
        z_relu, z_exp, elu_ready, z_hi, z_lo = (
            sem("z_relu"), sem("z_exp"), sem("elu_ready"), sem("z_hi"), sem("z_lo"))
        acc_used, acc_hi, acc_lo, fout_ready, fdiag_ready = (
            sem("acc_used"), sem("acc_hi"), sem("acc_lo"), sem("fout_ready"), sem("fdiag_ready"))
        frow_ready = sem("frow_ready")
        stats, veps_ready, rstd_ready, nmr_ready = (
            [sem(f"{n}{i}") for i in range(3)] for n in ("stats", "veps_ready", "rstd_ready", "nmr_ready"))
        h0_ready, relu_ready, ygamma, x1_ready, xb_ready = (
            sem("h0_ready"), sem("relu_ready"), sem("ygamma"),
            sem("x1_ready"), sem("xb_ready"))
        h1_ready, h1_hi, h1_lo, x1b_ready, out_ready = (
            sem("h1_ready"), sem("h1_hi"), sem("h1_lo"), sem("x1b_ready"), sem("out_ready"))

        x_tiles = x.rearrange("b (n p) f -> b p n f", p=P)
        out_tiles = out.rearrange("b (n p) f -> b p n f", p=P)

        def row(v):
            return v.rearrange("(a n) -> a n", a=1).broadcast_to((P, v.shape[0]))

        def flat(ap):
            return ap.rearrange("p a b -> p (a b)")

        def hl(t, *at):
            return [flat(t[(slice(None), i, *at)]) if not at else flat(t[:, i, at[0], :, :]) for i in range(2)]

        SPLITS = [
            (hl(W_hl), flat(score[0][:, :, :]), ld_W, 16 * FT),
            (hl(wa_hl), flat(wa[:, :, :]), wa_ready, 2 * FT * H),
            (hl(Wout_hl), flat(score[1][:, :, :]), ld_Wout, 16),
            (hl(w1_hl), flat(y[:, 0:2, :]), ld_small, 16 * SMALL_LOADS),
            (hl(w2_hl), flat(y[:, 2:4, :]), ld_small, 16 * SMALL_LOADS),
            (hl(wij_hl, 0), flat(ps_acc[:, 0:2, :]), L1_turned, 1),
            (hl(wij_hl, 1), flat(ps_acc[:, 2:4, :]), L1_turned, 1),
        ]
        FIRST_HALVES, HALVES = 2, len(SPLITS)

        block = ctx.enter_context(nc.Block())

        @block.sync
        def _(sp):
            sp.dma_start(xin[:, :, :], x_tiles[0]).then_inc(ld_x, 16)
            for k in range(FT):
                sp.dma_start(flat(score[0][:, :, :])[:, k * H * O:(k + 1) * H * O].rearrange("p (h o) -> p h o", o=O),
                             W_heads[:, k * P:(k + 1) * P, :].rearrange("h p o -> p h o")).then_inc(ld_W, 16)
            sp.dma_start(elu[:, :], row(a_heads[0:2, :].rearrange("h o -> (h o)"))).then_inc(ld_a, 16)
            sp.dma_start(h1f[:, :, :].rearrange("p n o -> p (n o)"),
                         row(a_heads[2:4, :].rearrange("h o -> (h o)"))).then_inc(ld_a, 16)
            sp.dma_start(score[2][:, :, :].bitcast(I32), adj.rearrange("(n p) j -> p n j", p=P)).then_inc(ld_adj, 16)
            sp.dma_start(score[1][:, :, :].rearrange("p a (b o) -> p (a b) o", o=O),
                         W_out.rearrange("(k p) o -> p k o", p=P)).then_inc(ld_Wout, 16)
            sp.dma_start(xres[:, :, :].rearrange("p (c a) o -> p c (a o)", c=FT),
                         L1_W.rearrange("(c p) d -> p c d", p=P)).then_inc(ld_L1, 16)
            sp.dma_start(y[:, 0:2, :], w1.rearrange("(k p) o -> p k o", p=P)).then_inc(ld_small, 16)
            sp.dma_start(y[:, 2:4, :], w2.rearrange("(k p) o -> p k o", p=P)).then_inc(ld_small, 16)
            with nc.allow_non_contiguous_dma(reason="one bias, once"):
                sp.dma_start(b1_col[:, :], b1.rearrange("(k p) -> p k", p=P)).then_inc(ld_small, 16)
            for dst, src in ((b2_row, b2), (gamma_row, gamma), (beta_row, beta), (bL_row, L1_b)):
                sp.dma_start(dst[:, :], row(src)).then_inc(ld_small, 16)
            sp.dma_start(aout_row[:, :, :].rearrange("p a o -> p (a o)"), row(a_out)).then_inc(ld_small, 16)

            def step(t):
                if exists(t, -2):
                    wait(sp, x1_ready, 4 * (t - 2))
                    sp.wait_ge(gen_evacuated, GEN_EVAC.after(t - 1, "ffn1"))
                    sp.wait_ge(L1_turned, 1)
                    sp.dma_start(xres[:, :, :], x_tiles[t - 2]).then_inc(ld_xres, 16)
                if exists(t, 2):
                    sp.wait_ge(gen_ready, GEN.after(t, "h0T"))
                    sp.dma_start(xin[:, :, :], x_tiles[t + 2]).then_inc(ld_x, 16)
                if exists(t, -2):
                    sp.wait_ge(out_ready, t - 1)
                    sp.dma_start(out_tiles[t - 2], h1f[:, :, :]).then_inc(st_out, 16)

            steps(sp, step)
            sp.wait_ge(st_out, 16 * B)

        @block.tensor
        def _(pe):
            mm = nc.tensor.matmul

            def split3(dst, stat, mov, first, last, **kw):
                mm(dst, stat[1], mov[0], start=first, stop=False, **kw)
                mm(dst, stat[0], mov[1], start=False, stop=False, **kw)
                return mm(dst, stat[0], mov[0], start=False, stop=last, **kw)

            def halves(ap_of):
                return ap_of(0), ap_of(1)

            def gen_claim(t, use, apart=False):
                names = list(GEN_USES)
                s, at = t, names.index(use)
                while True:
                    at -= 1
                    if at < 0:
                        s, at = s - 1, len(names) - 1
                    if isinstance(s, int) and s < FIRST_STEP:
                        return
                    if exists(s, GEN_USES[names[at]][0]):
                        break
                before = names[at]
                if before == "L1":
                    pe.wait_ge(out_ready, s - 1)
                elif apart:
                    wait_apart(pe, gen_evacuated, GEN_EVAC.after(s, before), ident_ready)
                else:
                    pe.wait_ge(gen_evacuated, GEN_EVAC.after(s, before))

            def turn(t, slot, c):
                if not has_unit(t, slot):
                    return
                n = unit_no(t, slot)
                if c == 0:
                    pe.wait_ge(probs_ready, 4 * n)
                    if has_unit(t, slot + 1):
                        pe.wait_ge(logits_ready, 4 * (n + 1))
                wait(pe, turned_lo, 4 * (n - 1) + c - 1)
                p = score[SCORE_BUFFER[slot % SLOTS]]
                for i in range(NT):
                    last = nc.tensor.transpose(ps_turn[:, c % 2, i * P:(i + 1) * P], p[:, i, c * P:(c + 1) * P], ident[:, :])
                last.then_inc(turned, 1)

            def attend(t, slot, c):
                if not has_unit(t, slot):
                    return
                n, head = unit_no(t, slot), HEAD_OF[slot]
                if c == 0:
                    wait(pe, elu_ready, n - 1)
                    if head is None:
                        pe.wait_ge(acc_lo, t)
                    else:
                        pe.wait_ge(gen_evacuated, GEN_EVAC.after(t - 1 if head in (1, 2) else t, f"value{head}"))
                pe.wait_ge(turned_lo, 4 * (n - 1) + c + 1)
                v = value_out if head is None else value[:, head % 2]
                for o in range(FT):
                    last = split3(ps_z[:, o, :],
                                  halves(lambda s: v[:, s, c, o * P:(o + 1) * P]),
                                  halves(lambda s: probT[:, c % 2, s, :]), c == 0, c == NT - 1)
                last.then_inc(chunk_used, 1)

            def values(t, head):
                if not exists(t, 0 if head == 3 else 1):
                    return
                gen_claim(t, f"value{head}")
                pe.wait_ge(gen_evacuated, GEN_EVAC.after(t - 1 if head == 3 else t, "h0T"))
                for j in range(NT):
                    for k in range(FT):
                        last = split3(gen_rows[:, j, :], halves(lambda s: h0T[:, s, k, j * P:(j + 1) * P]),
                                      halves(lambda s: W_hl[:, s, k, head * O:(head + 1) * O]), k == 0, k == FT - 1)
                last.then_inc(gen_ready, 1)

            def out_project(t, head):
                if not exists(t, 0):
                    return
                if head == 0:
                    wait(pe, acc_lo, t)
                    wait(pe, fout_ready, 8 * t)
                pe.wait_ge(z_lo, UNIT_Z(t, head))
                for j in range(NT):
                    for k in range(FT):
                        last = split3(ps_acc[:, j, :],
                                      halves(lambda s: zT[:, head % 2, s, k * N + j * P:k * N + (j + 1) * P]),
                                      halves(lambda s: Wout_hl[:, s, head * FT + k, :]),
                                      head == 0 and k == 0 and j % 2 == 0, head == H - 1 and k == FT - 1,
                                      skip_group_check=True)
                last.then_inc(acc_used, 1)

            def UNIT_Z(b, head):
                return unit_no(b - 1, 4) if head == 0 else unit_no(b, {1: 0, 2: 1, 3: 3}[head])

            def turn_h0(t, ahead=False):
                if not does_h0(t, ahead):
                    return
                gen_claim(t, "h0T")
                pe.wait_ge(h0_ready, 4 * (t + 2))
                for k in range(FT):
                    for i in range(NT):
                        last = nc.tensor.transpose(ps_gen[:, k, i * P:(i + 1) * P], xin[:, i, k * P:(k + 1) * P],
                                                   ident[:, :])
                last.then_inc(gen_ready, 1)

            def f_rows(t, ahead=False):
                if not does_h0(t, ahead):
                    return
                gen_claim(t, "frows")
                for k in range(FT):
                    last = split3(ps_gen[0:2 * H, 0, :], halves(lambda s: wa_hl[:, s, k, :]),
                                  halves(lambda s: h0T[:, s, k, :]), k == 0, k == FT - 1)
                last.then_inc(gen_ready, 1)

            def f1_columns(t, ahead=False):
                if not does_h0(t, ahead):
                    return
                gen_claim(t, "f1", apart=True)
                for i in range(NT):
                    last = nc.tensor.transpose(ps_gen[:, 0, i * 2 * H:(i + 1) * 2 * H], frow[:, i * P:(i + 1) * P],
                                               ident[0:2 * H, 0:2 * H])
                last.then_inc(gen_ready, 1)

            def broadcast(t, slot):
                if not has_unit(t, slot):
                    return
                n = unit_no(t, slot)
                before = unit_no(t, slot - 2)
                if has_unit(t, slot - 2):
                    pe.wait_ge(turned_lo, 4 * before - 1)
                else:
                    wait(pe, turned_lo, 4 * before)
                    wait(pe, logits_ready, 4 * (n - 1))
                head = HEAD_OF[slot % SLOTS]
                if head is None:
                    pe.wait_ge(fdiag_ready, 4 * t)
                    for j in range(NT):
                        last = mm(bcast[:, j * P:(j + 1) * P], ones[:, :], f2_diag[:, j, :], start=True, stop=True)
                else:
                    if head == 0:
                        pe.wait_ge(gen_evacuated, GEN_EVAC.after(t, "frows"))
                    last = mm(bcast, select[:, head, :], frow_hl[:, :], start=True, stop=True)
                last.then_inc(bcast_ready, 1)

            def ffn1(t):
                if not exists(t, -1):
                    return
                gen_claim(t, "ffn1")
                pe.wait_ge(z_lo, unit_no(t, 2))
                for m in range(FT):
                    for k in range(FT):
                        last = split3(ps_gen[:, m, :], halves(lambda s: w1_hl[:, s, k, m * P:(m + 1) * P]),
                                      halves(lambda s: oT[:, s, k * N:(k + 1) * N]), k == 0, k == FT - 1)
                last.then_inc(gen_ready, 1)

            def ffn2(t):
                if not exists(t, -2):
                    return
                gen_claim(t, "ffn2")
                for i in range(NT):
                    first = i % 2 == 0
                    for k in range(FT):
                        split3(gen_rows[:, i, :], halves(lambda s: rT[:, s, k * N + i * P:k * N + (i + 1) * P]),
                               halves(lambda s: w2_hl[:, s, k, :]), first and k == 0, False, skip_group_check=True)
                    for k in range(FT):
                        for s in range(2):
                            last = mm(gen_rows[:, i, k * P:(k + 1) * P], oT[:, s, k * N + i * P:k * N + (i + 1) * P],
                                      ident_r[:, :], start=False, stop=(s == 1 and k == FT - 1), skip_group_check=True)
                last.then_inc(gen_ready, 1)

            def adj_h(t):
                if not exists(t, -2):
                    return
                gen_claim(t, "AH")
                pe.wait_ge(h1_lo, t - 1)
                for d in range(FT):
                    for j in range(NT):
                        for s in (1, 0):
                            last = mm(ps_gen[:, d, :], h1[:, s, j, d * P:(d + 1) * P], adjT[:, j, :],
                                      start=(j == 0 and s == 1), stop=(j == NT - 1 and s == 0))
                last.then_inc(gen_ready, 1)

            def deg_h(t):
                if not exists(t, -2):
                    return
                if no_heads(t):
                    pe.wait_ge(fout_ready, 8 * B)
                else:
                    gen_claim(t, "DH")
                for d in range(FT):
                    for j in range(NT):
                        for s in (1, 0):
                            last = mm(dh_bank(t)[:, d * N + j * P:d * N + (j + 1) * P],
                                      h1[:, s, j, d * P:(d + 1) * P], deg_diag[:, j, :],
                                      start=(s == 1), stop=(s == 0))
                last.then_inc(gen_ready, 1)

            def layer1(t):
                if not exists(t, -2):
                    return
                gen_claim(t, "L1")
                for i in range(NT):
                    for m, src in ((1, rT), (0, dhT)):
                        for k in range(FT):
                            last = split3(gen_rows[:, i, :], halves(lambda s: src[:, s, k * N + i * P:k * N + (i + 1) * P]),
                                          halves(lambda s: wij_hl[:, s, m, k, :]), m == 1 and k == 0, m == 0 and k == FT - 1)
                last.then_inc(gen_ready, 1)

            pe.wait_ge(ident_ready, 1)
            turn_h0(FIRST_STEP, ahead=True)
            pe.wait_ge(const_ready, CONSTS)
            pe.wait_ge(halves_hi, FIRST_HALVES)
            pe.wait_ge(halves_lo, FIRST_HALVES)
            f_rows(FIRST_STEP, ahead=True)
            pe.wait_ge(adj_float, 1)
            for j in range(NT):
                bank = (ps_turn, ps_z)[j // 2][:, j % 2, :]
                for i in range(NT):
                    last = nc.tensor.transpose(bank[:, i * P:(i + 1) * P], score[2][:, i, j * P:(j + 1) * P], ident[:, :])
                last.then_inc(adj_turned, 1)
            f1_columns(FIRST_STEP, ahead=True)
            pe.wait_ge(ld_L1, 16)
            lw = xres[:, :, :].rearrange("p (c a) o -> p c (a o)", c=FT)
            for m in range(2):
                for d in range(FT):
                    for c in range(FT):
                        last = nc.tensor.transpose(ps_acc[:, 2 * m + d, c * P:(c + 1) * P],
                                                   lw[:, c, m * F + d * P:m * F + (d + 1) * P], ident[:, :])
            last.then_inc(L1_turned, 1)
            pe.wait_ge(exact_ready, NT + 2)

            def step(t):
                if isinstance(t, int) and t == FIRST_STEP + 1:
                    pe.wait_ge(halves_lo, HALVES)
                    pe.wait_ge(halves_hi, HALVES)
                    pe.wait_ge(deg_ready, 2)
                turn(t, 0, 2)
                attend(t, 0, 0)
                attend(t, 0, 1)
                turn(t, 0, 3)
                broadcast(t, 2)
                attend(t, 0, 2)
                ffn2(t)
                attend(t, 0, 3)
                turn(t, 1, 0)
                turn(t, 1, 1)
                values(t, 3)
                turn(t, 1, 2)
                attend(t, 1, 0)
                turn(t, 1, 3)
                attend(t, 1, 1)
                turn_h0(t)
                attend(t, 1, 2)
                broadcast(t, 3)
                out_project(t, 0)
                attend(t, 1, 3)
                turn(t, 2, 0)
                turn(t, 2, 1)
                f_rows(t)
                out_project(t, 1)
                turn(t, 2, 2)
                attend(t, 2, 0)
                turn(t, 2, 3)
                f1_columns(t)
                attend(t, 2, 1)
                broadcast(t, 4)
                attend(t, 2, 2)
                values(t, 0)
                attend(t, 2, 3)
                turn(t, 3, 0)
                turn(t, 3, 1)
                out_project(t, 2)
                adj_h(t)
                turn(t, 3, 2)
                attend(t, 3, 0)
                attend(t, 3, 1)
                turn(t, 3, 3)
                deg_h(t)
                broadcast(t, 5)
                attend(t, 3, 2)
                attend(t, 3, 3)
                layer1(t)
                turn(t, 4, 0)
                turn(t, 4, 1)
                values(t, 1)
                attend(t, 4, 0)
                turn(t, 4, 2)
                attend(t, 4, 1)
                turn(t, 4, 3)
                broadcast(t, 6)
                ffn1(t)
                out_project(t, 3)
                attend(t, 4, 2)
                attend(t, 4, 3)
                turn(t, 5, 0)
                turn(t, 5, 1)
                values(t, 2)

            def drain(t):
                ffn2(t)
                broadcast(t, 2)
                turn(t, 2, 0)
                turn(t, 2, 1)
                turn(t, 2, 2)
                attend(t, 2, 0)
                turn(t, 2, 3)
                attend(t, 2, 1)
                attend(t, 2, 2)
                attend(t, 2, 3)
                adj_h(t)
                deg_h(t)
                layer1(t)
                ffn1(t)

            steps(pe, step, drain)

        @block.scalar
        def _(act):
            def copy(dst, src):
                return nc.scalar.activation(dst, src, ACT.Copy)

            def gen_hi_copy(t, use, dst, src):
                act.wait_ge(gen_ready, GEN.after(t, use))
                copy(dst, src).then_inc(gen_hi, 1)

            def value_hi(t, head):
                if exists(t, 0 if head == 3 else 1):
                    gen_hi_copy(t, f"value{head}", value[:, head % 2, 0, :, :].rearrange("p n o -> p (n o)"), gen_flat)

            def f1_copy(t, ahead=False):
                if does_h0(t, ahead):
                    act.wait_ge(gen_ready, GEN.after(t, "f1"))
                    copy(f1[:, :, :].rearrange("p n c -> p (n c)"), ps_gen[:, 0, 0:NT * 2 * H]).then_inc(gen_evacuated, 1)

            def logits(t, slot, tiles=range(NT)):
                if not has_unit(t, slot):
                    return
                n, s = unit_no(t, slot), slot % SLOTS
                head = HEAD_OF[s]
                if tiles[0] == 0:
                    act.wait_ge(bcast_ready, n)
                    if isinstance(t, int) and t == FIRST_STEP and slot == 6:
                        act.wait_ge(halves_lo, 3)
                    if head is None:
                        act.wait_ge(fout_ready, 8 * t)
                    if head == 0:
                        act.wait_ge(gen_evacuated, GEN_EVAC.after(t, "f1"))
                    wait(act, turned, 4 * same_score_before(t, slot))
                for i in tiles:
                    bias = f_out[:, 0, i:i + 1] if head is None else f1[:, i, head:head + 1]
                    nc.scalar.activation(score[SCORE_BUFFER[s]][:, i, :], bcast, ACT.Identity, bias=bias)\
                        .then_inc(logits_ready, 1)

            def same_score_before(t, slot):
                for back in range(1, SLOTS + 1):
                    if SCORE_BUFFER[(slot - back) % SLOTS] == SCORE_BUFFER[slot % SLOTS]:
                        s = slot - back
                        return unit_no(t, s)
                return 0

            def exps(t, slot, tiles=range(NT)):
                if not has_unit(t, slot):
                    return
                n, s = unit_no(t, slot), slot % SLOTS
                if tiles[0] == 0:
                    act.wait_ge(negmax_ready, n)
                for i in tiles:
                    p = score[SCORE_BUFFER[s]][:, i, :]
                    nc.scalar.activation(p, p, ACT.Exp, bias=negmax[:, s, i:i + 1],
                                         accum_out=rowsum[:, s, i:i + 1]).then_inc(exp_done, 1)

            def turned_hi_copy(t, slot, c):
                if not has_unit(t, slot):
                    return
                k = 4 * (unit_no(t, slot) - 1) + c
                act.wait_ge(turned, k + 1)
                wait(act, chunk_used, k - 1)
                copy(probT[:, c % 2, 0, :], ps_turn[:, c % 2, :]).then_inc(turned_hi, 1)

            def elu_relu(t, slot):
                if not has_unit(t, slot):
                    return
                n = unit_no(t, slot)
                act.wait_ge(chunk_used, 4 * n)
                wait(act, z_lo, n - 1)
                nc.scalar.activation(elu[:, :], ps_z[:, :, :].rearrange("p a b -> p (a b)"), ACT.Relu,
                                     scale=-1.0).then_inc(z_relu, 1)

            def elu_exp(t, slot):
                if not has_unit(t, slot):
                    return
                n = unit_no(t, slot)
                act.wait_ge(z_relu, n)
                nc.scalar.activation(elu[:, :], elu[:, :], ACT.Exp, scale=-1.0).then_inc(z_exp, 1)

            def elu_hi(t, slot):
                if not has_unit(t, slot):
                    return
                n, head = unit_no(t, slot), HEAD_OF[slot]
                act.wait_ge(elu_ready, n)
                if head is None:
                    if exists(t, -2):
                        act.wait_ge(gen_ready, GEN.after(t, "ffn2"))
                    copy(oT[:, 0, :], elu[:, :]).then_inc(z_hi, 1)
                else:
                    wait(act, acc_used, 4 * (t + UNIT_BATCH[slot]) + head - 1)
                    copy(zT[:, head % 2, 0, :], elu[:, :]).then_inc(z_hi, 1)

            def acc_hi_copy(t):
                if exists(t, 0):
                    act.wait_ge(acc_used, 4 * (t + 1))
                    copy(value_out[:, 0, :, :], ps_acc[:, :, :]).then_inc(acc_hi, 1)

            def h0_relu(t, ahead=False):
                if not does_h0(t, ahead):
                    return
                act.wait_ge(nmr_ready[0], t + 2)
                for i in range(NT):
                    nc.scalar.activation(xin[:, i, :], xin[:, i, :], ACT.Relu, bias=nmr[:, 0, i:i + 1],
                                         scale=rstd[:, 0, i:i + 1]).then_inc(h0_ready, 1)

            def h1_relu(t):
                if not exists(t, -2):
                    return
                act.wait_ge(nmr_ready[2], t - 1)
                wait(act, st_out, 16 * (t - 2))
                for i in range(NT):
                    last = nc.scalar.activation(h1f[:, i, :], y[:, i, :], ACT.Relu, bias=nmr[:, 2, i:i + 1],
                                                scale=rstd[:, 2, i:i + 1])
                    last.then_inc(h1_ready, 1)
                act.wait_ge(h1_ready, 4 * (t - 1))
                copy(h1[:, 0, :, :], h1f[:, :, :]).then_inc(h1_hi, 1)

            def frow_copy(t, ahead=False):
                if not does_h0(t, ahead):
                    return
                act.wait_ge(gen_ready, GEN.after(t, "frows"))
                copy(frow_hl[0:2 * H, :], ps_gen[0:2 * H, 0, :]).then_inc(gen_hi, 1)
                copy(frow[:, :], ps_gen[0:2 * H, 0, :]).then_inc(frow_ready, 1)

            def ffn_relu(t):
                if not exists(t, -1):
                    return
                act.wait_ge(gen_ready, GEN.after(t, "ffn1"))
                for m in range(FT):
                    nc.scalar.activation(rF[:, m * N:(m + 1) * N], ps_gen[:, m, :], ACT.Relu,
                                         bias=b1_col[:, m:m + 1]).then_inc(relu_ready, 1)
                act.wait_ge(relu_ready, 2 * t)
                copy(rT[:, 0, :], rF[:, :]).then_inc(gen_hi, 1)

            def h0T_hi(t, ahead=False):
                if does_h0(t, ahead):
                    gen_hi_copy(t, "h0T", h0T[:, 0, :, :], ps_gen[:, :, :])

            def AH_hi(t):
                if exists(t, -2):
                    gen_hi_copy(t, "AH", rT[:, 0, :], gen_flat)

            def DH_hi(t):
                if exists(t, -2):
                    gen_hi_copy(t, "DH", dhT[:, 0, :], dh_bank(t))

            def split_hi(first, last):
                for dst, src, sem_, value_ in SPLITS[first:last]:
                    act.wait_ge(sem_, value_)
                    copy(dst[0], src).then_inc(halves_hi, 1)

            h0_relu(FIRST_STEP, ahead=True)
            split_hi(0, 1)
            h0T_hi(FIRST_STEP, ahead=True)
            split_hi(1, 2)
            act.wait_ge(ident_ready, 1)
            copy(ident_r[:, :], ident[:, :]).then_inc(exact_ready, 1)
            act.wait_ge(const_ready, CONSTS)
            copy(select[:, :, :], selectf).then_inc(exact_ready, 1)
            split_hi(2, 3)
            frow_copy(FIRST_STEP, ahead=True)
            for j in range(NT):
                act.wait_ge(adj_turned, j + 1)
                copy(adjT[:, j, :], (ps_turn, ps_z)[j // 2][:, j % 2, :]).then_inc(exact_ready, 1)
            f1_copy(FIRST_STEP, ahead=True)

            def later_weights(t):
                if isinstance(t, int) and t == FIRST_STEP:
                    split_hi(3, HALVES)

            def step(t):
                turned_hi_copy(t, 0, 2)
                exps(t, 1, (0, 1))
                turned_hi_copy(t, 0, 3)
                logits(t, 2, (0, 1))
                later_weights(t)
                exps(t, 1, (2, 3))
                logits(t, 2, (2, 3))
                h0_relu(t)
                elu_relu(t, 0)
                turned_hi_copy(t, 1, 0)
                elu_exp(t, 0)
                turned_hi_copy(t, 1, 1)
                value_hi(t, 3)
                exps(t, 2, (0, 1))
                turned_hi_copy(t, 1, 2)
                exps(t, 2, (2, 3))
                turned_hi_copy(t, 1, 3)
                h0T_hi(t)
                elu_hi(t, 0)
                logits(t, 3, (0, 1))
                logits(t, 3, (2, 3))
                elu_relu(t, 1)
                turned_hi_copy(t, 2, 0)
                elu_exp(t, 1)
                turned_hi_copy(t, 2, 1)
                frow_copy(t)
                exps(t, 3, (0, 1))
                exps(t, 3, (2, 3))
                turned_hi_copy(t, 2, 2)
                f1_copy(t)
                elu_hi(t, 1)
                turned_hi_copy(t, 2, 3)
                logits(t, 4, (0, 1))
                logits(t, 4, (2, 3))
                h1_relu(t)
                value_hi(t, 0)
                elu_relu(t, 2)
                turned_hi_copy(t, 3, 0)
                elu_exp(t, 2)
                exps(t, 4, (0, 1))
                turned_hi_copy(t, 3, 1)
                elu_hi(t, 2)
                AH_hi(t)
                turned_hi_copy(t, 3, 2)
                exps(t, 4, (2, 3))
                turned_hi_copy(t, 3, 3)
                DH_hi(t)
                logits(t, 5, (0, 1))
                logits(t, 5, (2, 3))
                elu_relu(t, 3)
                elu_exp(t, 3)
                turned_hi_copy(t, 4, 0)
                turned_hi_copy(t, 4, 1)
                exps(t, 5, (0, 1))
                elu_hi(t, 3)
                value_hi(t, 1)
                turned_hi_copy(t, 4, 2)
                exps(t, 5, (2, 3))
                turned_hi_copy(t, 4, 3)
                logits(t, 6, (0, 1))
                logits(t, 6, (2, 3))
                ffn_relu(t)
                acc_hi_copy(t)
                elu_relu(t, 4)
                turned_hi_copy(t, 5, 0)
                elu_exp(t, 4)
                turned_hi_copy(t, 5, 1)
                value_hi(t, 2)
                elu_hi(t, 4)

            def drain(t):
                logits(t, 2, (0, 1))
                logits(t, 2, (2, 3))
                exps(t, 2, (0, 1))
                exps(t, 2, (2, 3))
                turned_hi_copy(t, 2, 0)
                turned_hi_copy(t, 2, 1)
                h1_relu(t)
                turned_hi_copy(t, 2, 2)
                turned_hi_copy(t, 2, 3)
                AH_hi(t)
                DH_hi(t)
                elu_relu(t, 2)
                elu_exp(t, 2)
                elu_hi(t, 2)
                ffn_relu(t)

            steps(act, step, drain)

        @block.vector
        def _(dve):
            tt, ts, stt = nc.vector.tensor_tensor, nc.vector.tensor_scalar, nc.vector.scalar_tensor_tensor
            ttr = nc.vector.tensor_tensor_reduce

            def lo(dst, v, hi):
                return tt(dst, v, hi.bitcast(F32), ALU.subtract)

            def layer_norm(k, m, src_tiles):
                for i in range(NT):
                    nc.vector.bn_stats(bn[:, k, i, :], src_tiles[:, i, :]).then_inc(stats[k], 1)
                wait_apart(dve, stats[k], 8 * (m - 1) + 4, ident_ready)
                for i in range(NT):
                    nc.vector.bn_aggr(mv[:, k, i, :], bn[:, k, i, :]).then_inc(stats[k], 1)
                dve.wait_ge(stats[k], 8 * m)
                ts(veps[:, k, :], mv[:, k, :, 1], EPS, None, ALU.add).then_inc(veps_ready[k], 1)

            def negate_mean(t, k, ahead=False):
                if not (does_h0(t, ahead) if k == 0 else exists(t, -2)):
                    return
                m = t + 2 if k == 0 else t - 1
                dve.wait_ge(rstd_ready[k], m)
                stt(out=nmr[:, k, :], in0=mv[:, k, :, 0], scalar=-1.0, in1=rstd[:, k, :], op0=ALU.mult,
                    op1=ALU.mult).then_inc(nmr_ready[k], 1)

            def gen_lo(t, use, dst, src, hi):
                dve.wait_ge(gen_ready, GEN.after(t, use))
                dve.wait_ge(gen_hi, GEN_HI.after(t, use))
                lo(dst, src, hi).then_inc(gen_evacuated, 1)

            def value_lo(t, head):
                if exists(t, 0 if head == 3 else 1):
                    v = value[:, head % 2]
                    gen_lo(t, f"value{head}", flat(v[:, 1, :, :]), gen_flat, flat(v[:, 0, :, :]))

            def h0T_lo(t, ahead=False):
                if does_h0(t, ahead):
                    gen_lo(t, "h0T", h0T[:, 1, :, :], ps_gen[:, :, :], h0T[:, 0, :, :])

            def AH_lo(t):
                if exists(t, -2):
                    gen_lo(t, "AH", rT[:, 1, :], gen_flat, rT[:, 0, :])

            def DH_lo(t):
                if exists(t, -2):
                    gen_lo(t, "DH", dhT[:, 1, :], dh_bank(t), dhT[:, 0, :])

            def masks(t, slot, tiles):
                if not has_unit(t, slot):
                    return
                n, s = unit_no(t, slot), slot % SLOTS
                tile = score[SCORE_BUFFER[s]]
                for i in tiles:
                    dve.wait_ge(logits_ready, 4 * (n - 1) + i + 1)
                    stt(out=tile[:, i, :], in0=tile[:, i, :], scalar=SLOPE, in1=tile[:, i, :], op0=ALU.mult,
                        op1=ALU.max).then_inc(leaky_ready, 1)
                for i in tiles:
                    wait_apart(dve, leaky_ready, 4 * (n - 1) + i + 1, ident_ready)
                    ttr(out=tile[:, i, :], in0=tile[:, i, :], in1=mask[:, i, :], scale=1.0, scalar=LOWEST,
                        op0=ALU.add, op1=ALU.max, accum_out=rowmax[:, s, i:i + 1]).then_inc(masked_ready, 1)
                if i == NT - 1:
                    dve.wait_ge(masked_ready, 4 * n)
                    ts(negmax[:, s, :], rowmax[:, s, :], -1.0, None, ALU.mult).then_inc(negmax_ready, 1)

            def row_inverse(t, slot):
                if not has_unit(t, slot):
                    return
                n, s = unit_no(t, slot), slot % SLOTS
                dve.wait_ge(exp_done, 4 * n)
                nc.vector.reciprocal(rinv[:, s, :], rowsum[:, s, :]).then_inc(rinv_ready, 1)

            def turned_lo_copy(t, slot, c):
                if not has_unit(t, slot):
                    return
                k = 4 * (unit_no(t, slot) - 1) + c
                dve.wait_ge(turned_hi, k + 1)
                lo(probT[:, c % 2, 1, :], ps_turn[:, c % 2, :], probT[:, c % 2, 0, :]).then_inc(turned_lo, 1)

            def elu_last(t, slot):
                if not has_unit(t, slot):
                    return
                n = unit_no(t, slot)
                dve.wait_ge(z_exp, n)
                stt(out=elu[:, :], in0=elu[:, :], scalar=-1.0, in1=flat(ps_z[:, :, :]), op0=ALU.add,
                    op1=ALU.max).then_inc(elu_ready, 1)

            def acc_lo_copy(t):
                if exists(t, 0):
                    dve.wait_ge(acc_hi, t + 1)
                    lo(value_out[:, 1, :, :], ps_acc[:, :, :], value_out[:, 0, :, :]).then_inc(acc_lo, 1)

            def out_logit_parts(t, a):
                if not exists(t, 0):
                    return
                if a == 1:
                    dve.wait_ge(acc_hi, t + 1)
                    if exists(t, -1):
                        dve.wait_ge(logits_ready, 4 * unit_no(t, OUT_SLOT))
                for j in range(NT):
                    m = 8 * t + 4 * (1 - a) + j
                    wait(dve, fout_ready, m - 1)
                    ttr(out=scratch[:, j % 2, :], in0=ps_acc[:, j, :], in1=aout_row[:, a, :], scale=1.0, scalar=0.0,
                        op0=ALU.mult, op1=ALU.add, accum_out=f_out[:, a, j:j + 1]).then_inc(fout_ready, 1)

            def h0_stats(t, ahead=False):
                if not does_h0(t, ahead):
                    return
                dve.wait_ge(ld_x, 16 * (t + 2))
                layer_norm(0, t + 2, xin)

            def y_evacuate(t):
                if not exists(t, -2):
                    return
                dve.wait_ge(gen_ready, GEN.after(t, "ffn2"))
                wait(dve, out_ready, t - 2)
                tt(y[:, :, :], gen_rows, b2_row[:, :].unsqueeze(1).broadcast_to((P, NT, O)), ALU.add)\
                    .then_inc(gen_evacuated, 1)
                dve.wait_ge(gen_evacuated, GEN_EVAC.after(t, "ffn2"))
                layer_norm(1, t - 1, y)

            def x1_stats(t):
                if not exists(t, -2):
                    return
                dve.wait_ge(x1_ready, 4 * (t - 1))
                layer_norm(2, t - 1, y)

            def frow_lo(t, ahead=False):
                if not does_h0(t, ahead):
                    return
                dve.wait_ge(frow_ready, t + 2)
                gen_lo(t, "frows", frow_hl[32:32 + 2 * H, :], ps_gen[0:2 * H, 0, :], frow_hl[0:2 * H, :])

            def y_gamma(t):
                if exists(t, -2):
                    dve.wait_ge(veps_ready[1], t - 1)
                    for i in range(NT):
                        stt(out=y[:, i, :], in0=y[:, i, :], scalar=mv[:, 1, i, 0:1], in1=gamma_row[:, :],
                            op0=ALU.subtract, op1=ALU.mult).then_inc(ygamma, 1)

            def x1_sum(t):
                if exists(t, -2):
                    dve.wait_ge(rstd_ready[1], t - 1)
                    dve.wait_ge(xb_ready, t - 1)
                    dve.wait_ge(ygamma, 4 * (t - 1))
                    for i in range(NT):
                        stt(out=y[:, i, :], in0=y[:, i, :], scalar=rstd[:, 1, i:i + 1], in1=xres[:, i, :],
                            op0=ALU.mult, op1=ALU.add).then_inc(x1_ready, 1)

            def h1_lo_copy(t):
                if exists(t, -2):
                    dve.wait_ge(h1_hi, t - 1)
                    lo(h1[:, 1, :, :], h1f[:, :, :], h1[:, 0, :, :]).then_inc(h1_lo, 1)

            def add_bias(t):
                if exists(t, -2):
                    dve.wait_ge(h1_ready, 4 * (t - 1))
                    for i in range(NT):
                        stt(out=y[:, i, :], in0=bL_row[:, :], scalar=deg[:, i:i + 1], in1=y[:, i, :], op0=ALU.mult,
                            op1=ALU.add).then_inc(x1b_ready, 1)

            def result(t):
                if not exists(t, -2):
                    return
                dve.wait_ge(gen_ready, GEN.after(t, "L1"))
                dve.wait_ge(x1b_ready, 4 * (t - 1))
                dve.wait_ge(h1_lo, t - 1)
                tt(h1f[:, :, :], gen_rows, y[:, :, :], ALU.add).then_inc(out_ready, 1)

            def split_lo(first, last):
                for i, (dst, src, sem_, value_) in enumerate(SPLITS[first:last]):
                    dve.wait_ge(sem_, value_)
                    dve.wait_ge(halves_hi, first + i + 1)
                    lo(dst[1], src, dst[0]).then_inc(halves_lo, 1)

            h0_stats(FIRST_STEP, ahead=True)
            negate_mean(FIRST_STEP, 0, ahead=True)
            dve.wait_ge(ld_W, 16 * FT)
            dve.wait_ge(ld_a, 32)
            n = 0
            for h in range(H):
                a_rows = elu[:, :] if h < 2 else flat(h1f[:, :, :])
                for k in range(FT):
                    for a in range(2):
                        at = (h % 2) * 2 * O + a * O
                        wait(dve, wa_ready, n - 1)
                        ttr(out=scratch[:, n % 2, :], in0=flat(score[0][:, :, :])[:, (k * H + h) * O:(k * H + h + 1) * O],
                            in1=a_rows[:, at:at + O], scale=1.0, scalar=0.0, op0=ALU.mult, op1=ALU.add,
                            accum_out=wa[:, k, a * H + h:a * H + h + 1]).then_inc(wa_ready, 1)
                        n += 1
            split_lo(0, 2)
            h0T_lo(FIRST_STEP, ahead=True)
            dve.wait_ge(ld_adj, 16)
            nc.vector.tensor_copy(score[2][:, :, :], score[2][:, :, :].bitcast(I32)).then_inc(adj_float, 1)
            dve.wait_ge(adj_float, 1)
            ts(mask[:, :, :], score[2][:, :, :], 0.0, MASKED, ALU.is_le, ALU.mult)
            nc.vector.reduce_sum(deg[:, :], score[2][:, :, :], AX_X).then_inc(deg_ready, 1)
            dve.wait_ge(ident_ready, 1)
            dve.wait_ge(deg_ready, 1)
            for i in range(NT):
                last = ts(deg_diag[:, i, :], ident[:, :], deg[:, i:i + 1], None, ALU.mult)
            last.then_inc(deg_ready, 1)
            frow_lo(FIRST_STEP, ahead=True)

            def later_weights(t):
                if isinstance(t, int) and t == FIRST_STEP:
                    split_lo(2, HALVES)

            def step(t):
                later_weights(t)
                turned_lo_copy(t, 0, 2)
                h0_stats(t)
                turned_lo_copy(t, 0, 3)
                masks(t, 2, (0, 1))
                row_inverse(t, 1)
                negate_mean(t, 0)
                masks(t, 2, (2, 3))
                y_evacuate(t)
                turned_lo_copy(t, 1, 0)
                elu_last(t, 0)
                turned_lo_copy(t, 1, 1)
                value_lo(t, 3)
                y_gamma(t)
                turned_lo_copy(t, 1, 2)
                row_inverse(t, 2)
                x1_sum(t)
                h0T_lo(t)
                turned_lo_copy(t, 1, 3)
                masks(t, 3, (0, 1))
                masks(t, 3, (2, 3))
                turned_lo_copy(t, 2, 0)
                elu_last(t, 1)
                frow_lo(t)
                turned_lo_copy(t, 2, 1)
                x1_stats(t)
                row_inverse(t, 3)
                turned_lo_copy(t, 2, 2)
                negate_mean(t, 2)
                turned_lo_copy(t, 2, 3)
                masks(t, 4, (0, 1))
                masks(t, 4, (2, 3))
                h1_lo_copy(t)
                value_lo(t, 0)
                turned_lo_copy(t, 3, 0)
                elu_last(t, 2)
                add_bias(t)
                turned_lo_copy(t, 3, 1)
                AH_lo(t)
                turned_lo_copy(t, 3, 2)
                row_inverse(t, 4)
                turned_lo_copy(t, 3, 3)
                DH_lo(t)
                masks(t, 5, (0, 1))
                masks(t, 5, (2, 3))
                result(t)
                elu_last(t, 3)
                turned_lo_copy(t, 4, 0)
                turned_lo_copy(t, 4, 1)
                value_lo(t, 1)
                turned_lo_copy(t, 4, 2)
                row_inverse(t, 5)
                turned_lo_copy(t, 4, 3)
                masks(t, 6, (0, 1))
                masks(t, 6, (2, 3))
                out_logit_parts(t, 1)
                out_logit_parts(t, 0)
                turned_lo_copy(t, 5, 0)
                elu_last(t, 4)
                acc_lo_copy(t)
                turned_lo_copy(t, 5, 1)
                value_lo(t, 2)

            def drain(t):
                masks(t, 2, (0, 1))
                masks(t, 2, (2, 3))
                y_evacuate(t)
                row_inverse(t, 2)
                y_gamma(t)
                x1_sum(t)
                x1_stats(t)
                negate_mean(t, 2)
                turned_lo_copy(t, 2, 0)
                turned_lo_copy(t, 2, 1)
                turned_lo_copy(t, 2, 2)
                turned_lo_copy(t, 2, 3)
                h1_lo_copy(t)
                AH_lo(t)
                DH_lo(t)
                add_bias(t)
                elu_last(t, 2)
                result(t)

            steps(dve, step, drain)

        @block.gpsimd
        def _(pool):
            nc.gpsimd.memset(ident[:, :], 0.0).then_inc(zeroed, 1)
            nc.gpsimd.memset(selectf, 0.0).then_inc(zeroed, 1)
            nc.gpsimd.memset(frow_hl[:, :].bitcast(F32), 0.0).then_inc(const_ready, 1)
            nc.gpsimd.memset(ones[:, :], 1.0).then_inc(const_ready, 1)
            nc.gpsimd.memset(minus_half[:, :], -0.5).then_inc(const_ready, 1)
            pool.wait_ge(zeroed, 2)
            nc.gpsimd.affine_select(out=ident[:, :], in_=ident[:, :], compare_op=ALU.not_equal, fill=1.0, base=0,
                                    pattern=[[-1, P]], channel_multiplier=1).then_inc(ident_ready, 1)
            for n, first in enumerate((H, 32 + H)):
                pool.wait_ge(const_ready, 3 + n)
                nc.gpsimd.affine_select(out=selectf, in_=selectf, compare_op=ALU.not_equal, fill=1.0,
                                        base=-first, pattern=[[-1, H], [0, P]], channel_multiplier=1)\
                    .then_inc(const_ready, 1)

            def inverse_std(t, k, ahead=False):
                if not (does_h0(t, ahead) if k == 0 else exists(t, -2)):
                    return
                m = t + 2 if k == 0 else t - 1
                pool.wait_ge(veps_ready[k], m)
                nc.gpsimd.tensor_tensor(rstd[:, k, :], veps[:, k, :], minus_half[:, :], ALU.pow).then_inc(rstd_ready[k], 1)

            def normalise(t, slot):
                if not has_unit(t, slot):
                    return
                n, s = unit_no(t, slot), slot % SLOTS
                wait_apart(pool, rinv_ready, n, ident_ready)
                for i in range(NT):
                    p = score[SCORE_BUFFER[s]][:, i, :]
                    nc.gpsimd.tensor_scalar(p, p, rinv[:, s, i:i + 1], 1.0, ALU.mult, ALU.mult).then_inc(probs_ready, 1)

            def rows(v):
                return v[:, :].unsqueeze(1).broadcast_to((P, NT, O))

            def x_beta(t):
                if exists(t, -2):
                    pool.wait_ge(ld_small, 16 * SMALL_LOADS)
                    pool.wait_ge(ld_xres, 16 * (t - 1))
                    nc.gpsimd.tensor_tensor(xres[:, :, :], xres[:, :, :], rows(beta_row), ALU.add).then_inc(xb_ready, 1)

            def lo(dst, v, hi):
                return nc.gpsimd.tensor_tensor(dst, v, hi.bitcast(F32), ALU.subtract)

            def elu_lo(t, slot):
                if not has_unit(t, slot):
                    return
                n, head = unit_no(t, slot), HEAD_OF[slot]
                dst = oT if head is None else zT[:, head % 2]
                pool.wait_ge(z_hi, n)
                lo(dst[:, 1, :], elu[:, :], dst[:, 0, :]).then_inc(z_lo, 1)

            def ffn_lo(t):
                if exists(t, -1):
                    pool.wait_ge(gen_hi, GEN_HI.after(t, "ffn1"))
                    lo(rT[:, 1, :], rF[:, :], rT[:, 0, :]).then_inc(gen_evacuated, 1)

            def out_diagonal(t):
                if not exists(t, 0):
                    return
                if exists(t, -1):
                    pool.wait_ge(bcast_ready, unit_no(t, OUT_SLOT))
                wait_apart(pool, fout_ready, 8 * t + 4, ident_ready)
                for j in range(NT):
                    nc.gpsimd.tensor_scalar(f2_diag[:, j, :], ident[:, :], f_out[:, 1, j:j + 1], 1.0, ALU.mult,
                                            ALU.mult).then_inc(fdiag_ready, 1)

            inverse_std(FIRST_STEP, 0, ahead=True)

            def step(t):
                inverse_std(t, 0)
                x_beta(t)
                normalise(t, 1)
                inverse_std(t, 1)
                normalise(t, 2)
                elu_lo(t, 0)
                inverse_std(t, 2)
                normalise(t, 3)
                elu_lo(t, 1)
                elu_lo(t, 2)
                normalise(t, 4)
                elu_lo(t, 3)
                normalise(t, 5)
                ffn_lo(t)
                out_diagonal(t)
                elu_lo(t, 4)

            def drain(t):
                x_beta(t)
                inverse_std(t, 1)
                normalise(t, 2)
                inverse_std(t, 2)
                elu_lo(t, 2)
                ffn_lo(t)

            steps(pool, step, drain)


_INS = ['x', 'adj', 'L0_gnn_W_heads', 'L0_gnn_a_heads', 'L0_gnn_W_out', 'L0_gnn_a_out', 'L0_gnn_w1', 'L0_gnn_b1',
        'L0_gnn_w2', 'L0_gnn_b2', 'L0_gnn_ln_gamma', 'L0_gnn_ln_beta', 'L1_gnn_W', 'L1_gnn_b']


def kernel(**inputs):
    import numpy as np
    import concourse.bacc as bacc
    from concourse import mybir as mb
    from concourse.bass_utils import run_bass_kernel_spmd

    nc = bacc.Bacc("TRN2", target_bir_lowering=False, num_devices=1)
    arrays, args = {}, []
    for name in _INS:
        a = np.ascontiguousarray(inputs[name])
        arrays[f"in_{name}"] = a
        args.append(nc.dram_tensor(f"in_{name}", a.shape, mb.dt.from_np(a.dtype), kind="ExternalInput").ap())
    out = nc.dram_tensor("out", arrays["in_x"].shape, mb.dt.float32, kind="ExternalOutput").ap()
    build(nc, *args, out)
    r = run_bass_kernel_spmd(nc, [arrays], core_ids=[0])
    return r.results[0]["out"]
```
